# Optimizing a Trainium2 kernel written in Bass

```python
import numpy as np
import jax
import jax.numpy as jnp

def _softmax(x, axis=-1):
    return jax.nn.softmax(x, axis=axis)

def _gelu(x):
    return jax.nn.gelu(x, approximate=True)

def _silu(x):
    return jax.nn.silu(x)

def _sigmoid(x):
    return jax.nn.sigmoid(x)

def _layernorm(x, axis=-1, eps=1e-05):
    m = jnp.mean(x, axis=axis, keepdims=True)
    v = jnp.var(x, axis=axis, keepdims=True)
    return (x - m) / jnp.sqrt(v + eps)

def _scatter_add(tgt, idx, src, axis=0):
    return tgt.at[idx].add(src)

def _segment_sum(src, seg, n):
    return jax.ops.segment_sum(src, seg, n)
kernel_name = 'mk_vit_tower_d1_tok_img256_r4_e02c9c'

def setup_inputs(seed: int=0):
    np.random.seed(seed)
    _w = jnp.asarray

    def _rec_inputs():
        import jax
        import jax.numpy as jnp
        _rk = jax.random.key(seed)
        x = -0.000392918 + 0.999932 * jax.random.normal(jax.random.fold_in(_rk, 1), (4, 1, 128, 512), jnp.float32)
        return x
    x = _rec_inputs()

    def _L0_tok_setup():
        import jax, jax.numpy as jnp
        import numpy as np
        PATCH = 8
        EMBED = 64
        N_MELS = 128
        N_FRAMES = 512
        BATCH = 64
        NUM_PATCHES = N_MELS // PATCH * (N_FRAMES // PATCH)
        key = jax.random.key(seed)
        k1, k2, k3, k4 = jax.random.split(key, 4)
        x = jax.random.normal(k1, (BATCH, 1, N_MELS, N_FRAMES), dtype=jnp.float32)
        W = jax.random.normal(k2, (EMBED, PATCH * PATCH), dtype=jnp.float32) * (1.0 / np.sqrt(PATCH * PATCH))
        b = jax.random.normal(k3, (EMBED,), dtype=jnp.float32) * 0.01
        pos_embed = jax.random.normal(k4, (1, NUM_PATCHES, EMBED), dtype=jnp.float32) * 0.02
        return {'x': x, 'W': W, 'b': b, 'pos_embed': pos_embed}
    _L0_tok_all = _L0_tok_setup()
    _L0_tok_in = {k: v for k, v in _L0_tok_all.items() if k in ('W', 'b', 'pos_embed')}
    del _L0_tok_all

    def _L0_attn_setup():
        import jax, jax.numpy as jnp
        import numpy as np
        B, L, E = (2, 2048, 64)
        H, K, DIL = (8, 31, 2)
        DH = E // H

        def neighbor_indices(length, k, d):
            i = jnp.arange(length)
            g = i % d
            p = i // d
            lg = (length - g + d - 1) // d
            start = jnp.clip(p - k // 2, 0, lg - k)
            t = jnp.arange(k)
            return g[:, None] + (start[:, None] + t[None, :]) * d
        key = jax.random.key(seed)
        k0, k1, k2 = jax.random.split(key, 3)
        s = 0.02
        return {'x': jax.random.normal(k0, (B, L, E), jnp.float32), 'w_qkv': jax.random.normal(k1, (E, 3 * E), jnp.float32) * s, 'b_qkv': jnp.zeros((3 * E,), jnp.float32), 'w_proj': jax.random.normal(k2, (E, E), jnp.float32) * s, 'b_proj': jnp.zeros((E,), jnp.float32)}
    _L0_attn_all = _L0_attn_setup()
    _L0_attn_in = {k: v for k, v in _L0_attn_all.items() if k in ('w_qkv', 'b_qkv', 'w_proj', 'b_proj')}
    del _L0_attn_all

    def _L0_ffn_setup():
        import jax, jax.numpy as jnp
        import numpy as np
        D_MODEL = 64
        N_EXPERTS = 16
        HIDDEN = 128
        SCALE = 0.02
        key = jax.random.key(seed)
        ks = jax.random.split(key, 5)
        x = jax.random.normal(ks[0], (4, 2048, D_MODEL), dtype=jnp.float32)
        gate_w = jax.random.normal(ks[1], (D_MODEL, N_EXPERTS), dtype=jnp.float32) * SCALE
        gate_b = jnp.zeros((N_EXPERTS,), dtype=jnp.float32)
        w1 = jax.random.normal(ks[2], (N_EXPERTS, D_MODEL, HIDDEN), dtype=jnp.float32) * SCALE
        w2 = jax.random.normal(ks[3], (N_EXPERTS, D_MODEL, HIDDEN), dtype=jnp.float32) * SCALE
        w3 = jax.random.normal(ks[4], (N_EXPERTS, HIDDEN, D_MODEL), dtype=jnp.float32) * SCALE
        return {'x': x, 'gate_w': gate_w, 'gate_b': gate_b, 'w1': w1, 'w2': w2, 'w3': w3}
    _L0_ffn_all = _L0_ffn_setup()
    _L0_ffn_in = {k: v for k, v in _L0_ffn_all.items() if k in ('gate_w', 'gate_b', 'w1', 'w2', 'w3')}
    del _L0_ffn_all
    return {'x': x, 'L0_tok_W': _L0_tok_in['W'], 'L0_tok_b': _L0_tok_in['b'], 'L0_tok_pos_embed': _L0_tok_in['pos_embed'], 'L0_attn_w_qkv': _L0_attn_in['w_qkv'], 'L0_attn_b_qkv': _L0_attn_in['b_qkv'], 'L0_attn_w_proj': _L0_attn_in['w_proj'], 'L0_attn_b_proj': _L0_attn_in['b_proj'], 'L0_ffn_gate_w': _L0_ffn_in['gate_w'], 'L0_ffn_gate_b': _L0_ffn_in['gate_b'], 'L0_ffn_w1': _L0_ffn_in['w1'], 'L0_ffn_w2': _L0_ffn_in['w2'], 'L0_ffn_w3': _L0_ffn_in['w3']}

def reference(x, L0_tok_W, L0_tok_b, L0_tok_pos_embed, L0_attn_w_qkv, L0_attn_b_qkv, L0_attn_w_proj, L0_attn_b_proj, L0_ffn_gate_w, L0_ffn_gate_b, L0_ffn_w1, L0_ffn_w2, L0_ffn_w3):
    import jax
    import jax.numpy as jnp

    def _L0_tok_ref(x, W, b, pos_embed):
        import jax, jax.numpy as jnp
        import numpy as np
        PATCH = 8
        EMBED = 64
        N_MELS = 128
        N_FRAMES = 512
        BATCH = 64
        NUM_PATCHES = N_MELS // PATCH * (N_FRAMES // PATCH)
        B = x.shape[0]
        mp, fp = (N_MELS // PATCH, N_FRAMES // PATCH)
        xs = x[:, 0]
        patches = xs.reshape(B, mp, PATCH, fp, PATCH).transpose(0, 1, 3, 2, 4).reshape(B, mp * fp, PATCH * PATCH)
        emb = jnp.einsum('bnk,ek->bne', patches, W) + b
        return emb + pos_embed

    def _L0_attn_ref(x, w_qkv, b_qkv, w_proj, b_proj):
        import jax, jax.numpy as jnp
        import numpy as np
        B, L, E = (2, 2048, 64)
        H, K, DIL = (8, 31, 2)
        DH = E // H

        def neighbor_indices(length, k, d):
            i = jnp.arange(length)
            g = i % d
            p = i // d
            lg = (length - g + d - 1) // d
            start = jnp.clip(p - k // 2, 0, lg - k)
            t = jnp.arange(k)
            return g[:, None] + (start[:, None] + t[None, :]) * d
        b, l, e = x.shape
        qkv = (x @ w_qkv + b_qkv).reshape(b, l, 3, H, DH)
        q, k, v = (qkv[:, :, 0], qkv[:, :, 1], qkv[:, :, 2])
        nbr = neighbor_indices(l, K, DIL)
        kg = k[:, nbr]
        vg = v[:, nbr]
        scale = DH ** (-0.5)
        attn = jnp.einsum('blhd,blkhd->blhk', q, kg) * scale
        attn = jax.nn.softmax(attn, axis=-1)
        out = jnp.einsum('blhk,blkhd->blhd', attn, vg).reshape(b, l, e)
        return out @ w_proj + b_proj

    def _L0_ffn_ref(x, gate_w, gate_b, w1, w2, w3):
        import jax, jax.numpy as jnp
        import numpy as np
        D_MODEL = 64
        N_EXPERTS = 16
        HIDDEN = 128
        SCALE = 0.02
        n_experts = w1.shape[0]
        logits = jnp.einsum('bsd,de->bse', x, gate_w) + gate_b
        probs = jax.nn.softmax(logits, axis=-1)
        top_probs, top_idx = jax.lax.top_k(probs, 2)
        top_probs = top_probs / jnp.sum(top_probs, axis=-1, keepdims=True)
        dispatch = jnp.sum(jax.nn.one_hot(top_idx, n_experts, dtype=x.dtype) * top_probs[..., None], axis=-2)
        h1 = jnp.einsum('bsd,edh->bseh', x, w1)
        h2 = jnp.einsum('bsd,edh->bseh', x, w2)
        hidden = jax.nn.silu(h1) * h2
        expert_out = jnp.einsum('bseh,eho->bseo', hidden, w3)
        return jnp.einsum('bseo,bse->bso', expert_out, dispatch)
    h = _L0_tok_ref(x, L0_tok_W, L0_tok_b, L0_tok_pos_embed)
    h = h + _L0_attn_ref(_layernorm(h, axis=-1), L0_attn_w_qkv, L0_attn_b_qkv, L0_attn_w_proj, L0_attn_b_proj)
    h = h + _L0_ffn_ref(_layernorm(h, axis=-1), L0_ffn_gate_w, L0_ffn_gate_b, L0_ffn_w1, L0_ffn_w2, L0_ffn_w3)
    return h

_drawn_inputs = setup_inputs


def setup_inputs(seed=0):
    import zlib

    import numpy as np

    out = dict(_drawn_inputs(seed))
    spreads = {'L0_attn_b_qkv': (0.0, 0.417), 'L0_attn_b_proj': (0.0, 0.1), 'L0_ffn_gate_b': (0.0, 0.8)}
    factors = {'L0_tok_b': 6.168,
     'L0_tok_pos_embed': 2.915,
     'L0_attn_w_qkv': 8.0,
     'L0_attn_w_proj': 3.029,
     'L0_ffn_gate_w': 8.0,
     'L0_ffn_w1': 8.0,
     'L0_ffn_w2': 8.0,
     'L0_ffn_w3': 8.0}
    for name, (base, spread) in spreads.items():
        noise = np.random.default_rng([zlib.crc32(name.encode()), seed]).standard_normal(out[name].shape)
        drawn = base * np.exp(spread * noise) if base else spread * noise
        out[name] = jnp.asarray(drawn.astype(out[name].dtype))
    for name, factor in factors.items():
        out[name] = (out[name] * factor).astype(out[name].dtype)
    return out
```

```python
from contextlib import ExitStack

import concourse.bass as bass
from concourse import mybir

ALU = mybir.AluOpType
ACT = mybir.ActivationFunctionType
AX_X = mybir.AxisListType.X
F32 = mybir.dt.float32
F32R = mybir.dt.float32r
BF16 = mybir.dt.bfloat16
I32 = mybir.dt.int32
U32 = mybir.dt.uint32

SLOTS = 32
EPS = 1e-5
MASKED = -1e30
RSQRT_SEED = float(0x5F3759DF)
NEWTON = 3


def vit_tower(nc, x, tok_W, tok_b, pos_embed, w_qkv, b_qkv, w_proj, b_proj, gate_w, gate_b, w1, w2, w3, out):
    IMAGES, _, MELS, FRAMES = x.shape
    E = tok_W.shape[0]
    PATCH = 8
    ROWS, COLS = MELS // PATCH, FRAMES // PATCH // 2
    CHUNKS = 2 * IMAGES
    T = ROWS * COLS
    TILES = T // 128
    H, DH, K = 8, E // 8, 31
    G = T // 32
    SPAN = 32 + K - 1
    SCALE = float(DH) ** -0.5
    X, HID = gate_w.shape[1], w1.shape[2]
    PAIRS = X // 2
    PARTS = 3 * X

    def span_start(j):
        return min(max(32 * j - K // 2, 0), T - SPAN)

    with ExitStack() as ctx:
        def sb(name, shape, dt=F32):
            return ctx.enter_context(nc.sbuf_tensor(name, shape, dt))

        def bank(name):
            return ctx.enter_context(nc.psum_tensor(name, [128, 512], F32))

        def sem(name):
            return ctx.enter_context(nc.semaphore(name))

        ident = sb("ident", [128, 128])
        ident_bf = sb("ident_bf", [128, 128], BF16)
        fold = sb("fold", [128, E])
        mask = sb("mask", [128, 3, H, SPAN], BF16)
        edge = sb("edge", [128, H, SPAN])
        band = sb("band", [128, H, SPAN])
        spread = sb("spread", [128, PAIRS, 2, 64], BF16)
        iota_x = sb("iota_x", [128, X])
        tokW = sb("tokW", [E, 64])
        tokWT = sb("tokWT", [65, E])
        pos = sb("pos", [128, TILES, 2, E])
        Wqkv = sb("Wqkv", [65, 3 * E])
        Wproj = sb("Wproj", [65, E])
        gate = sb("gate", [128, X])
        gate_bias = sb("gate_bias", [128, X])
        w12 = sb("w12", [128, 2, X, HID])
        w_hi = sb("w_hi", [128, 2, X, HID], F32R)
        w_lo = sb("w_lo", [128, 2, X, HID], F32R)
        w3s = sb("w3s", [HID, X, E])

        x_stage = sb("x_stage", [128, FRAMES])
        by_frame = sb("by_frame", [COLS, 128, PATCH])
        patchT = sb("patchT", [65, T])
        tokens = sb("tokens", [128, 2, TILES, E])
        xn1 = sb("xn1", [128, TILES, E])
        xn1T = sb("xn1T", [65, T])
        qT = sb("qT", [128, T])
        kT = sb("kT", [128, T])
        k_diag = sb("k_diag", [128, H, T])
        v_span = sb("v_span", [128, G, H, DH + 1])
        smax = sb("smax", [128, TILES, H])
        probs = sb("probs", [128, TILES, H, SPAN])
        probsT = sb("probsT", [128, 2, H // 2, 128])
        inv_sum = sb("inv_sum", [128, TILES, H])
        attn = sb("attn", [128, TILES, E])
        attnT = sb("attnT", [65, T])
        resid = sb("resid", [128, 2, TILES, E])
        xn2 = sb("xn2", [128, TILES, E])
        xn2_parts = sb("xn2_parts", [128, TILES, 2 * E], F32R)
        x2T = sb("x2T", [128, 2, T], F32R)
        logits = sb("logits", [128, TILES, X])
        top = sb("top", [128, TILES, 8])
        top_at = sb("top_at", [128, TILES, 8], U32)
        top_idx = sb("top_idx", [128, TILES, 2])
        top_diff = sb("top_diff", [128, TILES, 2])
        top_exp = sb("top_exp", [128, TILES, 2])
        top_sum = sb("top_sum", [128, TILES])
        top_inv = sb("top_inv", [128, TILES])
        top_w = sb("top_w", [128, TILES, 2])
        hot_w = sb("hot_w", [128, 2, TILES, X])
        disp = sb("disp", [128, 2, TILES, X])
        disp_parts = sb("disp_parts", [128, TILES, PARTS], BF16)
        dispT = sb("dispT", [128, T], BF16)
        ln = [{"stats": sb(f"stats{n}", [128, TILES, 6]), "mv": sb(f"mv{n}", [128, TILES, 2]),
               "var": sb(f"var{n}", [128, TILES]), "half": sb(f"half{n}", [128, TILES]),
               "bits": sb(f"bits{n}", [128, TILES], I32), "y": sb(f"y{n}", [128, TILES], I32),
               "t": sb(f"t{n}", [128, TILES])} for n in (1, 2)]
        silu = sb("silu", [128, 2, T])
        hidden = sb("hidden", [128, 4, T])
        weight = sb("weight", [128, 2, T])
        y_w = sb("y_w", [128, 2, T])
        y_sum = sb("y_sum", [128, T])
        result = sb("result", [128, 2, TILES, E])

        b_h1, b_h2, b_y, b_w = bank("b_h1"), bank("b_h2"), bank("b_y"), bank("b_w")
        b_s, b_m = bank("b_s"), bank("b_m")
        b_p = [bank("b_p0"), bank("b_p1")]

        c_zero, c_tri, c_mask = sem("c_zero"), sem("c_tri"), sem("c_mask")
        c_ready, c_rows = sem("c_ready"), sem("c_rows")
        pe_apart, dve_apart, pool_apart = sem("pe_apart"), sem("dve_apart"), sem("pool_apart")
        d_tok, d_attn, d_ffn = sem("d_tok"), sem("d_attn"), sem("d_ffn")
        w_turned, w_copied = sem("w_turned"), sem("w_copied")
        hi_split, lo_split = sem("hi_split"), sem("lo_split")
        x_loaded, x_turned = sem("x_loaded"), sem("x_turned")
        frames_copied, patch_turned, patch_copied = sem("frames_copied"), sem("patch_turned"), sem("patch_copied")
        embedded, tokens_made = sem("embedded"), sem("tokens_made")
        ln_dve = [sem("ln1_dve"), sem("ln2_dve")]
        ln_newton = [sem("ln1_newton"), sem("ln2_newton")]
        xn1_made, xn1_turned, xn1_copied = sem("xn1_made"), sem("xn1_turned"), sem("xn1_copied")
        qk_made, v_made, q_copied, k_copied, v_copied = (
            sem("qk_made"), sem("v_made"), sem("q_copied"), sem("k_copied"), sem("v_copied"))
        k_spread = sem("k_spread")
        scored, maxed, centred = sem("scored"), sem("maxed"), sem("centred")
        exped = sem("exped")
        p_turned, p_copied, pv_done = sem("p_turned"), sem("p_copied"), sem("pv_done")
        inverted, attn_made, attn_turned, attn_copied = (
            sem("inverted"), sem("attn_made"), sem("attn_turned"), sem("attn_copied"))
        projected, resid_made = sem("projected"), sem("resid_made")
        xn2_made, hi_made, lo_made = sem("xn2_made"), sem("hi_made"), sem("lo_made")
        x2_turned, x2_copied = sem("x2_turned"), sem("x2_copied")
        gated, biased, topped, top_found, idx_made, diffed, top_exped = (
            sem("gated"), sem("biased"), sem("topped"), sem("top_found"), sem("idx_made"), sem("diffed"),
            sem("top_exped"))
        summed2, inverted2, weighed = sem("summed2"), sem("inverted2"), sem("weighed")
        routed = sem("routed")
        disp_turned, disp_copied = sem("disp_turned"), sem("disp_copied")
        h1_done, h2_done, silu_done, hid_done = sem("h1_done"), sem("h2_done"), sem("silu_done"), sem("hid_done")
        y_done, w_done, w_held, yw_done = sem("y_done"), sem("w_done"), sem("w_held"), sem("yw_done")
        summed = sem("summed")
        folded, result_made = sem("folded"), sem("result_made")
        stored = [sem("stored0"), sem("stored1")]
        ROUTE, LN5, NEWT = 6, 5, 1 + 4 * NEWTON

        def cid(chunk):
            return 2 * chunk[0] + chunk[1]

        def wait(eng, s, n):
            if not isinstance(n, int) or n > 0:
                eng.wait_ge(s, n)

        apart = {nc.tensor.engine: pe_apart, nc.vector.engine: dve_apart, nc.gpsimd.engine: pool_apart}

        def wait_apart(eng, s, n):
            wait(eng, s, n)
            if not isinstance(n, int):
                eng.sem_inc(apart[eng.engine], 1)

        def run_pipeline(eng, step, last):
            step(embed=(0, 0))
            step(embed=(0, 1), attend=(0, 0))
            step(embed=(1, 0), attend=(0, 1), experts=(0, 0))
            with eng.Fori(1, IMAGES) as b:
                step(embed=(b, 1), attend=(b, 0), experts=(b - 1, 1), finish=(b - 1, 0))
                step(embed=(b + 1, 0), attend=(b, 1), experts=(b, 0), finish=(b - 1, 1))
            step(experts=(IMAGES - 1, 1), finish=(IMAGES - 1, 0))
            last((IMAGES - 1, 1))

        block = ctx.enter_context(nc.Block())

        @block.sync
        def _(sp):
            sp.dma_start(x_stage[:], x[0, 0]).then_inc(x_loaded, 16)
            sp.dma_start(tokW[:], tok_W).then_inc(d_tok, 16)
            sp.dma_start(tokWT[64:65, :], tok_b.rearrange("(a e) -> a e", a=1)).then_inc(d_tok, 16)
            sp.dma_start(pos[:], pos_embed[0].rearrange("(t p g) e -> p t g e", t=TILES, g=2)).then_inc(d_tok, 16)
            sp.dma_start(Wqkv[0:E, :], w_qkv).then_inc(d_attn, 16)
            sp.dma_start(Wqkv[64:65, :], b_qkv.rearrange("(a e) -> a e", a=1)).then_inc(d_attn, 16)
            sp.dma_start(Wproj[0:E, :], w_proj).then_inc(d_attn, 16)
            sp.dma_start(Wproj[64:65, :], b_proj.rearrange("(a e) -> a e", a=1)).then_inc(d_attn, 16)
            for half in range(2):
                sp.dma_start(gate[64 * half:64 * half + 64, :], gate_w).then_inc(d_attn, 16)
            sp.dma_start(gate_bias[:], gate_b.partition_broadcast(128)).then_inc(d_attn, 16)

            def load_image(b):
                sp.wait_ge(x_turned, 2 * b)
                sp.dma_start(x_stage[:], x[b, 0]).then_inc(x_loaded, 16)

            def spread_keys(chunk):
                sp.wait_ge(k_copied, cid(chunk) + 1)
                for h in range(H):
                    sp.dma_start(k_diag[DH * h:DH * h + DH, h, :],
                                 kT[64 + DH * h:64 + DH * h + DH, :]).then_inc(k_spread, 16)

            def store(chunk):
                b, g = chunk
                sp.wait_ge(result_made, cid(chunk) + 1)
                sp.dma_start(out[b].rearrange("(t p g) e -> g p t e", t=TILES, g=2)[g],
                             result[:, g]).then_inc(stored[g], 16)

            spread_keys((0, 0))
            load_image(1)
            spread_keys((0, 1))
            with sp.Fori(1, IMAGES - 1) as b:
                spread_keys((b, 0))
                store((b - 1, 0))
                load_image(b + 1)
                spread_keys((b, 1))
                store((b - 1, 1))
            spread_keys((IMAGES - 1, 0))
            store((IMAGES - 2, 0))
            sp.wait_ge(x_turned, 2 * IMAGES)
            sp.dma_start(x_stage[:], x[0, 0]).then_inc(x_loaded, 16)
            spread_keys((IMAGES - 1, 1))
            store((IMAGES - 2, 1))
            store((IMAGES - 1, 0))
            store((IMAGES - 1, 1))
            for g in range(2):
                sp.wait_ge(stored[g], 16 * IMAGES)
            sp.wait_ge(x_loaded, 16 * (IMAGES + 1))

        @block.gpsimd
        def _(pool):
            for n in range(2):
                for half in range(2):
                    pool.dma_start(w12[64 * half:64 * half + 64, n],
                                   (w1, w2)[n].rearrange("e d h -> d e h")).then_inc(d_ffn, 16)
            pool.dma_start(w3s[:], w3.rearrange("e h o -> h e o")).then_inc(d_ffn, 16)

            pool.memset(ident[:], 0.0)
            pool.memset(fold[:], 0.0)
            pool.memset(spread[:], 0.0).then_inc(c_zero, 1)
            pool.wait_ge(c_zero, 1)
            pool.affine_select(out=ident[:], in_=ident[:], compare_op=ALU.not_equal, fill=1.0, base=0,
                               pattern=[[-1, 128]], channel_multiplier=1).then_inc(c_tri, 1)
            pool.affine_select(out=fold[:], in_=fold[:], compare_op=ALU.not_equal, fill=1.0, base=0,
                               pattern=[[-1, E]], channel_multiplier=1).then_inc(c_tri, 1)
            pool.wait_ge(c_tri, 2)
            pool.affine_select(out=fold[:], in_=fold[:], compare_op=ALU.not_equal, fill=1.0, base=-E,
                               pattern=[[-1, E]], channel_multiplier=1).then_inc(c_tri, 1)
            pool.tensor_copy(ident_bf[:], ident[:]).then_inc(c_tri, 1)
            pool.memset(k_diag[:], 0.0).then_inc(c_zero, 1)
            pool.wait_ge(c_zero, 2)

            steps = [0]

            def keep(t, h0, cond, base, mult, step, fill, rows=slice(0, 128)):
                if steps[0]:
                    pool.wait_ge(c_mask, steps[0])
                pool.affine_select(out=t[rows], in_=t[rows], compare_op=ALU.is_ge, fill=fill, base=base,
                                   pattern=[[0, H], [step, SPAN]], channel_multiplier=mult).then_inc(c_mask, 1)
                steps[0] += 1

            def step_done(ins):
                ins.then_inc(c_mask, 1)
                steps[0] += 1

            for g in range(4):
                rows = slice(32 * g, 32 * g + 32)
                if g == 0:
                    step_done(pool.memset(band[:], 0.0))
                keep(band, 0, None, 0, -1, 1, MASKED, rows)
                keep(band, 0, None, K - 1, 1, -1, MASKED, rows)
            for n in range(3):
                pool.wait_ge(c_mask, steps[0])
                step_done(pool.tensor_copy(mask[:, n], band[:]))
            first, lastg = slice(0, 32), slice(96, 128)
            pool.wait_ge(c_mask, steps[0])
            step_done(pool.memset(edge[:], 0.0))
            keep(edge, 0, None, K - 1, 0, -1, MASKED, first)
            keep(edge, 0, None, -(K // 2 + 1), -1, 1, 0.0, first)
            keep(edge, 0, None, K // 2, -1, 1, MASKED, first)
            keep(edge, 0, None, -(SPAN - K), 0, 1, MASKED, lastg)
            keep(edge, 0, None, K // 2 - 1, 1, -1, 0.0, lastg)
            keep(edge, 0, None, K // 2 + K - 1, 1, -1, MASKED, lastg)
            pool.wait_ge(c_mask, steps[0])
            step_done(pool.tensor_copy(mask[first, 0], edge[first]))
            step_done(pool.tensor_copy(mask[lastg, 2], edge[lastg]))
            for part in range(3):
                pool.wait_ge(c_mask, steps[0])
                step_done(pool.affine_select(out=spread[:], in_=spread[:], compare_op=ALU.not_equal, fill=1.0,
                                             base=-X * part, pattern=[[-2, PAIRS], [-1, 2], [0, 64]],
                                             channel_multiplier=1))
            pool.iota(iota_x[:], pattern=[[1, X]], base=0, channel_multiplier=0,
                      allow_small_or_imprecise_dtypes=True).then_inc(c_ready, 1)
            pool.wait_ge(c_mask, steps[0])
            pool.wait_ge(c_tri, 4)
            pool.engine_nop().then_inc(c_ready, 1)

            def newton(n, c):
                d, s = ln[n], ln_newton[n]
                y = d["y"][:].bitcast(F32)
                wait_apart(pool, ln_dve[n], LN5 * c + 5)
                pool.tensor_scalar(d["half"][:], d["var"][:], -0.5, None, ALU.mult).then_inc(s, 1)
                pool.wait_ge(s, NEWT * c + 1)
                for r in range(NEWTON):
                    at = NEWT * c + 1 + 4 * r
                    pool.tensor_tensor(d["t"][:], y, y, ALU.mult).then_inc(s, 1)
                    pool.wait_ge(s, at + 1)
                    pool.tensor_tensor(d["t"][:], d["t"][:], d["half"][:], ALU.mult).then_inc(s, 1)
                    wait_apart(pool, s, at + 2)
                    pool.tensor_scalar(d["t"][:], d["t"][:], 1.5, None, ALU.add).then_inc(s, 1)
                    pool.wait_ge(s, at + 3)
                    pool.tensor_tensor(y, y, d["t"][:], ALU.mult).then_inc(s, 1)
                    if r < NEWTON - 1:
                        pool.wait_ge(s, at + 4)

            def route(c):
                pool.wait_ge(idx_made, c + 1)
                wait_apart(pool, weighed, c + 1)
                for k in range(2):
                    for t in range(TILES):
                        ins = pool.tensor_scalar(hot_w[:, k, t], iota_x[:], top_idx[:, t, k:k + 1],
                                                 top_w[:, t, k:k + 1], ALU.is_equal, ALU.mult)
                ins.then_inc(routed, 1)
                pool.wait_ge(routed, ROUTE * c + 1)
                pool.tensor_tensor(disp[:, 0], hot_w[:, 0], hot_w[:, 1], ALU.add).then_inc(routed, 1)
                wait(pool, disp_turned, c)
                for k in range(2):
                    part = disp_parts[:, :, X * k:X * k + X]
                    wait_apart(pool, routed, ROUTE * c + 2 + 2 * k)
                    pool.tensor_copy(part, disp[:, k]).then_inc(routed, 1)
                    pool.wait_ge(routed, ROUTE * c + 3 + 2 * k)
                    rest = disp[:, 1] if k == 0 else disp_parts[:, :, 2 * X:3 * X]
                    pool.tensor_tensor(rest, disp[:, k], part, ALU.subtract).then_inc(routed, 1)

            def add_pair(c, q):
                pool.wait_ge(yw_done, PAIRS * c + q + 1)
                if q == 1:
                    wait(pool, folded, c)
                    pool.tensor_tensor(y_sum[:], y_w[:, 0], y_w[:, 1], ALU.add).then_inc(summed, 1)
                else:
                    pool.wait_ge(summed, (PAIRS - 1) * c + q - 1)
                    pool.tensor_tensor(y_sum[:], y_sum[:], y_w[:, q % 2], ALU.add).then_inc(summed, 1)

            def step(embed=None, attend=None, experts=None, finish=None):
                for s in range(SLOTS):
                    if s == 1 and finish is not None:
                        add_pair(cid(finish), PAIRS - 1)
                    if experts is not None and s % 4 == 1 and s > 5:
                        add_pair(cid(experts), (s - 5) // 4)
                    if s == 7 and embed is not None:
                        newton(0, cid(embed))
                    if s == 23 and attend is not None:
                        newton(1, cid(attend))
                    if s == 31 and attend is not None:
                        route(cid(attend))

            run_pipeline(pool, step, lambda chunk: add_pair(cid(chunk), PAIRS - 1))

        @block.tensor
        def _(pe):
            pe.wait_ge(c_ready, 2)
            pe.wait_ge(c_rows, 2)
            pe.wait_ge(d_tok, 48)
            pe.transpose(b_s[0:64, 0:E], tokW[:], ident[0:E, 0:E]).then_inc(w_turned, 1)

            def turn_frames(chunk):
                b, g = chunk
                c = cid(chunk)
                pe.wait_ge(x_loaded, 16 * b + 16)
                wait(pe, q_copied, c)
                wait(pe, k_copied, c)
                wait(pe, v_copied, 2 * c)
                cols = x_stage[:].rearrange("r (f g j) -> r g j f", g=2, j=PATCH)[:, g]
                for j in range(PATCH):
                    ins = pe.transpose(b_p[j // 4][0:COLS, 128 * (j % 4):128 * (j % 4) + 128], cols[:, j],
                                       ident[:])
                ins.then_inc(x_turned, 1)

            def turn_patches(chunk):
                c = cid(chunk)
                pe.wait_ge(frames_copied, c + 1)
                wait(pe, disp_copied, c - 1)
                wait_apart(pe, result_made, c - 2)
                for m in range(ROWS):
                    ins = pe.transpose(b_m[0:64, COLS * m:COLS * m + COLS],
                                       by_frame[:, PATCH * m:PATCH * m + PATCH].rearrange("f i j -> f (i j)"),
                                       ident[0:COLS, 0:COLS])
                ins.then_inc(patch_turned, 1)

            def embed_patches(chunk):
                c = cid(chunk)
                if isinstance(c, int) and c == 0:
                    pe.wait_ge(w_copied, 1)
                pe.wait_ge(patch_copied, c + 1)
                for t in range(TILES):
                    ins = pe.matmul(b_m[:, E * t:E * t + E], patchT[:, 128 * t:128 * t + 128], tokWT[:],
                                    start=True, stop=True)
                ins.then_inc(embedded, 1)

            def turn_xn1(chunk):
                wait_apart(pe, xn1_made, cid(chunk) + 1)
                for t in range(TILES):
                    ins = pe.transpose(b_m[0:E, 128 * t:128 * t + 128], xn1[:, t], ident[:])
                ins.then_inc(xn1_turned, 1)

            def make_qkv(chunk):
                c = cid(chunk)
                if isinstance(c, int) and c == 0:
                    pe.wait_ge(d_attn, 16 * 7)
                pe.wait_ge(xn1_copied, c + 1)
                wait(pe, p_copied, 2 * TILES * c)
                pe.matmul(b_p[0][:], Wqkv[:, 0:2 * E], xn1T[:], start=True, stop=True).then_inc(qk_made, 1)
                wait(pe, x2_copied, c)
                for half, dst in enumerate((b_p[1], b_s)):
                    for j in range(G // 2):
                        k0 = span_start(G // 2 * half + j)
                        ins = pe.matmul(dst[0:SPAN, E * j:E * j + E], xn1T[:, k0:k0 + SPAN],
                                        Wqkv[:, 2 * E:3 * E], start=True, stop=True)
                    ins.then_inc(v_made, 1)

            def score(chunk, t):
                c = cid(chunk)
                dst = (b_s, b_p[0], b_p[1], b_s)[t]
                if t == 0:
                    pe.wait_ge(k_spread, 16 * H * (c + 1))
                    pe.wait_ge(q_copied, c + 1)
                    pe.wait_ge(v_copied, 2 * (c + 1))
                if t == 1:
                    pe.wait_ge(k_copied, c + 1)
                    pe.wait_ge(frames_copied, c + 2)
                if t == 3:
                    pe.wait_ge(centred, TILES * c + 1)
                dst = dst[:, 0:H * SPAN]
                which = 0 if t == 0 else 2 if t == TILES - 1 else 1
                pe.matmul(dst, ident_bf[:], mask[:, which].rearrange("p h k -> p (h k)"), start=True, stop=False,
                          skip_group_check=True)
                for g in range(4):
                    k0 = span_start(4 * t + g)
                    ins = pe.matmul(dst[32 * g:32 * g + 32, :], qT[:, 128 * t + 32 * g:128 * t + 32 * g + 32],
                                    k_diag[:, :, k0:k0 + SPAN], start=False, stop=True, skip_group_check=True)
                ins.then_inc(scored, 1)

            def turn_probs(chunk, u):
                c = cid(chunk)
                if u == 0:
                    pe.wait_ge(exped, c + 1)
                    wait_apart(pe, centred, TILES * c + 3)
                if u >= 2:
                    wait_apart(pe, p_copied, 2 * TILES * c + u - 1)
                for k in range(H // 2):
                    ins = pe.transpose(b_p[u % 2][0:SPAN, 128 * k:128 * k + 128],
                                       probs[:, u // 2, H // 2 * (u % 2) + k], ident[:])
                ins.then_inc(p_turned, 1)

            def apply_probs(chunk, u):
                c = cid(chunk)
                t = u // 2
                pe.wait_ge(p_copied, 2 * TILES * c + u + 1)
                if u == 0:
                    pe.wait_ge(xn1_copied, c + 2)
                o = b_m[:, 0:TILES * H * (DH + 1)].rearrange("p (t h d) -> p t h d", t=TILES, h=H)
                for k in range(H // 2):
                    h = H // 2 * (u % 2) + k
                    for g in range(4):
                        ins = pe.matmul(o[32 * g:32 * g + 32, t, h], probsT[:, u % 2, k, 32 * g:32 * g + 32],
                                        v_span[:, 4 * t + g, h], start=True, stop=True)
                ins.then_inc(pv_done, 1)

            def turn_attn(chunk):
                pe.wait_ge(attn_made, cid(chunk) + 1)
                wait_apart(pe, centred, TILES * (cid(chunk) + 1))
                for t in range(TILES):
                    ins = pe.transpose(b_s[0:E, 128 * t:128 * t + 128], attn[:, t], ident[:])
                ins.then_inc(attn_turned, 1)

            def project(chunk):
                pe.wait_ge(attn_copied, cid(chunk) + 1)
                for t in range(TILES):
                    ins = pe.matmul(b_m[:, E * t:E * t + E], attnT[:, 128 * t:128 * t + 128], Wproj[:],
                                    start=True, stop=True)
                ins.then_inc(projected, 1)

            def turn_x2(chunk):
                pe.wait_ge(hi_made, cid(chunk) + 1)
                pe.wait_ge(lo_made, cid(chunk) + 1)
                for t in range(TILES):
                    ins = pe.transpose(b_s[:, 128 * t:128 * t + 128], xn2_parts[:, t].bitcast(F32), ident[:])
                ins.then_inc(x2_turned, 1)

            def make_logits(chunk):
                b, g = chunk
                pe.wait_ge(x2_copied, cid(chunk) + 1)
                for t in range(TILES):
                    ins = pe.matmul(b_m[:, X * t:X * t + X], x2T[:, g, 128 * t:128 * t + 128].bitcast(F32),
                                    gate[:], start=True, stop=True)
                ins.then_inc(gated, 1)

            def turn_disp(chunk):
                wait_apart(pe, routed, ROUTE * (cid(chunk) + 1))
                dst = b_m[:].bitcast(BF16)
                for t in range(TILES):
                    ins = pe.transpose(dst[0:PARTS, 128 * t:128 * t + 128], disp_parts[:, t], ident_bf[:])
                ins.then_inc(disp_turned, 1)

            def up(chunk, e):
                b, g = chunk
                c = cid(chunk)
                if e == 0:
                    pe.wait_ge(x2_copied, c + 1)
                    if isinstance(c, int) and c == 0:
                        pe.wait_ge(hi_split, 2)
                        pe.wait_ge(lo_split, 2)
                for n, (dst, free, made) in enumerate(((b_h1, silu_done, h1_done), (b_h2, hid_done, h2_done))):
                    wait(pe, free, X * c + e)
                    pe.matmul(dst[:], w_hi[:, n, e], x2T[:, g], start=True, stop=False)
                    pe.matmul(dst[:], w_lo[:, n, e], x2T[:, g], start=False, stop=True).then_inc(made, 1)

            def down(chunk, q):
                c = cid(chunk)
                pe.wait_ge(hid_done, X * c + 2 * q + 2)
                wait(pe, yw_done, PAIRS * c + q)
                for k in range(2):
                    ins = pe.matmul(b_y[64 * k:64 * k + 64, :], w3s[:, 2 * q + k], hidden[:, (2 * q + k) % 4],
                                    start=True, stop=True)
                ins.then_inc(y_done, 1)

            def spread_weights(chunk, q):
                c = cid(chunk)
                if q == 0:
                    pe.wait_ge(disp_copied, c + 1)
                wait(pe, w_held, PAIRS * c + q)
                pe.matmul(b_w[:], spread[:, q].rearrange("p a b -> p (a b)"), dispT[:], start=True,
                          stop=True).then_inc(w_done, 1)

            def fold_pairs(chunk):
                c = cid(chunk)
                pe.wait_ge(summed, (PAIRS - 1) * (c + 1))
                pe.wait_ge(disp_copied, min(c + 2, CHUNKS) if isinstance(c, int) else c + 2)
                for t in range(TILES):
                    ins = pe.matmul(b_m[:, E * t:E * t + E], y_sum[:, 128 * t:128 * t + 128], fold[:],
                                    start=True, stop=True)
                ins.then_inc(folded, 1)

            def step(embed=None, attend=None, experts=None, finish=None):
                for s in range(SLOTS):
                    if experts is not None:
                        if s % 2 == 0:
                            up(experts, s // 2)
                        if s % 4 == 3:
                            spread_weights(experts, (s - 3) // 4)
                        if s % 4 == 1 and s >= 5:
                            down(experts, (s - 5) // 4)
                    if finish is not None and s == 1:
                        down(finish, PAIRS - 1)
                    if experts is not None and s == 1:
                        turn_disp(experts)
                    if finish is not None and s == 3:
                        fold_pairs(finish)
                    if attend is not None:
                        if s == 0:
                            make_qkv(attend)
                    if embed is not None:
                        if s == 2:
                            turn_frames(embed)
                        if s == 5:
                            turn_patches(embed)
                        if s == 7:
                            embed_patches(embed)
                        if s == 11:
                            turn_xn1(embed)
                    if attend is not None:
                        if 4 <= s < 4 + TILES:
                            score(attend, s - 4)
                        if 12 <= s < 12 + 2 * TILES:
                            apply_probs(attend, s - 12)
                        if 10 <= s < 10 + 2 * TILES:
                            turn_probs(attend, s - 10)
                        if s == 21:
                            turn_attn(attend)
                        if s == 23:
                            project(attend)
                        if s == 27:
                            turn_x2(attend)
                        if s == 28:
                            make_logits(attend)

            def last(chunk):
                down(chunk, PAIRS - 1)
                fold_pairs(chunk)

            run_pipeline(pe, step, last)

        @block.scalar
        def _(act):
            act.wait_ge(c_rows, 2)
            act.wait_ge(w_turned, 1)
            nc.scalar.copy(tokWT[0:64, :], b_s[0:64, 0:E]).then_inc(w_copied, 1)

            def copy_frames(chunk):
                c = cid(chunk)
                act.wait_ge(x_turned, c + 1)
                wait(act, patch_turned, c)
                for k in range(2):
                    ins = nc.scalar.copy(by_frame[:, :, 4 * k:4 * k + 4].rearrange("f r j -> f j r"),
                                         b_p[k][0:COLS, :].rearrange("f (j r) -> f j r", j=4))
                ins.then_inc(frames_copied, 1)

            def copy_patches(chunk):
                c = cid(chunk)
                act.wait_ge(patch_turned, c + 1)
                wait(act, embedded, c)
                nc.scalar.copy(patchT[0:64, :], b_m[0:64, :]).then_inc(patch_copied, 1)

            def copy_xn1(chunk):
                c = cid(chunk)
                act.wait_ge(xn1_turned, c + 1)
                wait(act, v_made, 2 * c)
                nc.scalar.copy(xn1T[0:E, :], b_m[0:E, :]).then_inc(xn1_copied, 1)

            def copy_qk(chunk):
                c = cid(chunk)
                act.wait_ge(qk_made, c + 1)
                wait(act, k_spread, 16 * H * c)
                nc.scalar.copy(kT[64:128, :], b_p[0][64:128, :]).then_inc(k_copied, 1)
                nc.scalar.mul(qT[0:64, :], b_p[0][0:64, :], SCALE).then_inc(q_copied, 1)

            def exp_scores(chunk):
                c = cid(chunk)
                act.wait_ge(centred, TILES * (c + 1))
                flat = probs[:].rearrange("p t h k -> p (t h k)")
                nc.scalar.activation(flat, flat, ACT.Exp).then_inc(exped, 1)

            def copy_probs(chunk, u):
                n = 2 * TILES * cid(chunk) + u
                act.wait_ge(p_turned, n + 1)
                wait(act, pv_done, n - 1)
                nc.scalar.copy(probsT[0:SPAN, u % 2].rearrange("p h q -> p (h q)"),
                               b_p[u % 2][0:SPAN, :]).then_inc(p_copied, 1)

            def copy_attn(chunk):
                act.wait_ge(attn_turned, cid(chunk) + 1)
                nc.scalar.copy(attnT[0:E, :], b_s[0:E, :]).then_inc(attn_copied, 1)

            def copy_x2(chunk):
                b, g = chunk
                act.wait_ge(x2_turned, cid(chunk) + 1)
                nc.scalar.copy(x2T[:, g], b_s[:]).then_inc(x2_copied, 1)

            def exp_top(chunk):
                act.wait_ge(diffed, cid(chunk) + 1)
                nc.scalar.activation(top_exp[:], top_diff[:], ACT.Exp).then_inc(top_exped, 1)

            def copy_disp(chunk):
                c = cid(chunk)
                act.wait_ge(disp_turned, c + 1)
                wait(act, w_done, PAIRS * c)
                nc.scalar.copy(dispT[0:PARTS, :], b_m[:].bitcast(BF16)[0:PARTS, 0:T]).then_inc(disp_copied, 1)

            def silu_up(chunk, e):
                n = X * cid(chunk) + e
                act.wait_ge(h1_done, n + 1)
                wait(act, hid_done, n - 1)
                nc.scalar.activation(silu[:, e % 2], b_h1[:], ACT.Silu).then_inc(silu_done, 1)

            def hold_weights(chunk, q):
                n = PAIRS * cid(chunk) + q
                act.wait_ge(w_done, n + 1)
                wait(act, yw_done, n - 1)
                nc.scalar.copy(weight[:, q % 2], b_w[:]).then_inc(w_held, 1)

            def step(embed=None, attend=None, experts=None, finish=None):
                for s in range(SLOTS):
                    if experts is not None:
                        if s % 2 == 0:
                            silu_up(experts, s // 2)
                        if s % 4 == 3:
                            hold_weights(experts, (s - 3) // 4)
                        if s == 1:
                            copy_disp(experts)
                    if embed is not None:
                        if s == 2:
                            copy_frames(embed)
                        if s == 5:
                            copy_patches(embed)
                        if s == 11:
                            copy_xn1(embed)
                    if attend is not None:
                        if s == 0:
                            copy_qk(attend)
                        if s == 8:
                            exp_scores(attend)
                        if 10 <= s < 10 + 2 * TILES:
                            copy_probs(attend, s - 10)
                        if s == 21:
                            copy_attn(attend)
                        if s == 27:
                            copy_x2(attend)
                        if s == 30:
                            exp_top(attend)
                if attend is not None and experts is None:
                    act.wait_ge(d_ffn, 16 * 5)
                    for n in range(2):
                        nc.scalar.copy(w_hi[:, n].rearrange("p e h -> p (e h)"),
                                       w12[:, n].rearrange("p e h -> p (e h)")).then_inc(hi_split, 1)

            run_pipeline(act, step, lambda chunk: None)

        @block.vector
        def _(dve):
            nc.vector.memset(patchT[64:65, :], 1.0)
            nc.vector.memset(xn1T[64:65, :], 1.0)
            nc.vector.memset(attnT[64:65, :], 1.0)
            nc.vector.memset(qT[64:128, :], 0.0)
            nc.vector.memset(v_span[:], 0.0).then_inc(c_rows, 1)
            nc.vector.memset(probsT[:], 0.0)
            nc.vector.memset(dispT[:], 0.0)
            dve.wait_ge(c_rows, 1)
            nc.vector.memset(v_span[:, :, :, DH:DH + 1], 1.0).then_inc(c_rows, 1)
            dve.wait_ge(c_ready, 2)
            dve.wait_ge(d_tok, 48)
            dve.wait_ge(d_attn, 16 * 7)

            def stats(n, src, c):
                d, s = ln[n], ln_dve[n]
                for t in range(TILES):
                    ins = nc.vector.bn_stats(d["stats"][:, t], src[:, t])
                ins.then_inc(s, 1)
                wait_apart(dve, s, LN5 * c + 1)
                for t in range(TILES):
                    ins = nc.vector.bn_aggr(d["mv"][:, t], d["stats"][:, t])
                ins.then_inc(s, 1)
                dve.wait_ge(s, LN5 * c + 2)
                nc.vector.tensor_scalar(d["var"][:], d["mv"][:, :, 1], EPS, None, ALU.add).then_inc(s, 1)
                dve.wait_ge(s, LN5 * c + 3)
                nc.vector.tensor_scalar(d["bits"][:], d["var"][:].bitcast(I32), 1, None,
                                        ALU.logical_shift_right).then_inc(s, 1)
                dve.wait_ge(s, LN5 * c + 4)
                nc.vector.tensor_scalar(d["y"][:], d["bits"][:], -1.0, RSQRT_SEED, ALU.mult,
                                        ALU.add).then_inc(s, 1)

            def normalise(n, dst, src, c, made):
                d = ln[n]
                dve.wait_ge(ln_newton[n], NEWT * (c + 1))
                for t in range(TILES):
                    ins = nc.vector.tensor_scalar(dst[:, t], src[:, t], d["mv"][:, t, 0:1],
                                                  d["y"][:, t:t + 1].bitcast(F32), ALU.subtract, ALU.mult)
                ins.then_inc(made, 1)

            def make_tokens(chunk):
                b, g = chunk
                c = cid(chunk)
                dve.wait_ge(embedded, c + 1)
                nc.vector.tensor_tensor(tokens[:, g], b_m[:, 0:TILES * E].rearrange("p (t e) -> p t e", t=TILES),
                                        pos[:, :, g], ALU.add).then_inc(tokens_made, 1)
                dve.wait_ge(tokens_made, c + 1)
                stats(0, tokens[:, g], c)

            def normalise1(chunk):
                b, g = chunk
                c = cid(chunk)
                wait(dve, xn1_turned, c)
                normalise(0, xn1, tokens[:, g], c, xn1_made)

            def copy_v(chunk):
                c = cid(chunk)
                wait(dve, pv_done, 2 * TILES * c)
                for half, src in enumerate((b_p[1], b_s)):
                    dve.wait_ge(v_made, 2 * c + half + 1)
                    nc.vector.tensor_copy(
                        v_span[0:SPAN, G // 2 * half:G // 2 * (half + 1), :, 0:DH],
                        src[0:SPAN, :].rearrange("p (j h d) -> p j h d", h=H, d=DH)).then_inc(v_copied, 1)

            def centre(chunk, t):
                n = TILES * cid(chunk) + t
                src = (b_s, b_p[0], b_p[1], b_s)[t][:, 0:H * SPAN].rearrange("p (h k) -> p h k", h=H)
                dve.wait_ge(scored, n + 1)
                nc.vector.tensor_reduce(smax[:, t], src, AX_X, ALU.max).then_inc(maxed, 1)
                if t == 0:
                    wait(dve, p_turned, 2 * n)
                dve.wait_ge(maxed, n + 1)
                nc.vector.tensor_tensor(probs[:, t], src,
                                        smax[:, t].unsqueeze(2).to_broadcast([128, H, SPAN]),
                                        ALU.subtract).then_inc(centred, 1)

            def divide(chunk):
                c = cid(chunk)
                dve.wait_ge(pv_done, 2 * TILES * (c + 1))
                o = b_m[:, 0:TILES * H * (DH + 1)].rearrange("p (th d) -> p th d", d=DH + 1)
                nc.vector.reciprocal(inv_sum[:].rearrange("p t h -> p (t h)"), o[:, :, DH]).then_inc(inverted, 1)
                dve.wait_ge(inverted, c + 1)
                nc.vector.tensor_tensor(
                    attn[:].rearrange("p t (h d) -> p (t h) d", d=DH), o[:, :, 0:DH],
                    inv_sum[:].rearrange("p t h -> p (t h)").unsqueeze(2).to_broadcast([128, TILES * H, DH]),
                    ALU.mult).then_inc(attn_made, 1)

            def add_attention(chunk):
                b, g = chunk
                c = cid(chunk)
                dve.wait_ge(projected, c + 1)
                nc.vector.tensor_tensor(resid[:, g], b_m[:, 0:TILES * E].rearrange("p (t e) -> p t e", t=TILES),
                                        tokens[:, g], ALU.add).then_inc(resid_made, 1)
                dve.wait_ge(resid_made, c + 1)
                stats(1, resid[:, g], c)

            def normalise2(chunk):
                b, g = chunk
                c = cid(chunk)
                normalise(1, xn2, resid[:, g], c, xn2_made)
                dve.wait_ge(xn2_made, c + 1)
                nc.vector.tensor_copy(xn2_parts[:, :, 0:E], xn2[:]).then_inc(hi_made, 1)
                dve.wait_ge(hi_made, c + 1)
                nc.vector.tensor_tensor(xn2_parts[:, :, E:2 * E], xn2[:], xn2_parts[:, :, 0:E].bitcast(F32),
                                        ALU.subtract).then_inc(lo_made, 1)

            def pick_top(chunk):
                c = cid(chunk)
                dve.wait_ge(gated, c + 1)
                nc.vector.tensor_tensor(
                    logits[:], b_m[:, 0:TILES * X].rearrange("p (t x) -> p t x", t=TILES),
                    gate_bias[:].unsqueeze(1).to_broadcast([128, TILES, X]), ALU.add).then_inc(biased, 1)
                wait_apart(dve, biased, c + 1)
                for t in range(TILES):
                    ins = nc.vector.max(top[:, t], logits[:, t])
                ins.then_inc(topped, 1)
                dve.wait_ge(topped, c + 1)
                nc.vector.tensor_tensor(top_diff[:], top[:, :, 0:2],
                                        top[:, :, 0:1].to_broadcast([128, TILES, 2]),
                                        ALU.subtract).then_inc(diffed, 1)
                for t in range(TILES):
                    ins = nc.vector.max_index(top_at[:, t], top[:, t], logits[:, t])
                ins.then_inc(top_found, 1)
                dve.wait_ge(top_found, c + 1)
                wait(dve, routed, ROUTE * c)
                nc.vector.tensor_copy(top_idx[:], top_at[:, :, 0:2]).then_inc(idx_made, 1)

            def weigh_top(chunk):
                c = cid(chunk)
                dve.wait_ge(top_exped, c + 1)
                nc.vector.tensor_tensor(top_sum[:], top_exp[:, :, 0], top_exp[:, :, 1], ALU.add).then_inc(summed2, 1)
                dve.wait_ge(summed2, c + 1)
                nc.vector.reciprocal(top_inv[:], top_sum[:]).then_inc(inverted2, 1)
                dve.wait_ge(inverted2, c + 1)
                nc.vector.tensor_tensor(top_w[:], top_exp[:],
                                        top_inv[:].unsqueeze(2).to_broadcast([128, TILES, 2]),
                                        ALU.mult).then_inc(weighed, 1)

            def gate_hidden(chunk, e):
                n = X * cid(chunk) + e
                dve.wait_ge(silu_done, n + 1)
                dve.wait_ge(h2_done, n + 1)
                wait(dve, y_done, PAIRS * cid(chunk) + e // 2 - 1)
                nc.vector.tensor_tensor(hidden[:, e % 4], silu[:, e % 2], b_h2[:], ALU.mult).then_inc(hid_done, 1)

            def weigh_pair(chunk, q):
                c = cid(chunk)
                n = PAIRS * c + q
                dve.wait_ge(y_done, n + 1)
                dve.wait_ge(w_held, n + 1)
                wait(dve, summed, (PAIRS - 1) * c + (q - 1 if q < 2 else max(q - 2, 1)))
                nc.vector.tensor_tensor(y_w[:, q % 2], b_y[:], weight[:, q % 2], ALU.mult).then_inc(yw_done, 1)

            def make_result(chunk):
                b, g = chunk
                c = cid(chunk)
                dve.wait_ge(folded, c + 1)
                wait(dve, stored[g], 16 * b)
                nc.vector.tensor_tensor(result[:, g], b_m[:, 0:TILES * E].rearrange("p (t e) -> p t e", t=TILES),
                                        resid[:, g], ALU.add).then_inc(result_made, 1)

            def step(embed=None, attend=None, experts=None, finish=None):
                for s in range(SLOTS):
                    if finish is not None:
                        if s == 1:
                            weigh_pair(finish, PAIRS - 1)
                        if s == 3:
                            make_result(finish)
                    if experts is not None:
                        if s % 2 == 0:
                            gate_hidden(experts, s // 2)
                        if s % 4 == 1 and s >= 5:
                            weigh_pair(experts, (s - 5) // 4)
                    if attend is not None:
                        if s == 0:
                            copy_v(attend)
                        if 4 <= s < 4 + TILES:
                            centre(attend, s - 4)
                    if embed is not None:
                        if s == 7:
                            make_tokens(embed)
                        if s == 10:
                            normalise1(embed)
                    if attend is not None:
                        if s == 19:
                            divide(attend)
                        if s == 23:
                            add_attention(attend)
                        if s == 26:
                            normalise2(attend)
                        if s == 28:
                            pick_top(attend)
                        if s == 31:
                            weigh_top(attend)
                if attend is not None and experts is None:
                    for n in range(2):
                        dve.wait_ge(hi_split, n + 1)
                        nc.vector.tensor_tensor(w_lo[:, n], w12[:, n], w_hi[:, n].bitcast(F32),
                                                ALU.subtract).then_inc(lo_split, 1)

            def last(chunk):
                weigh_pair(chunk, PAIRS - 1)
                make_result(chunk)

            run_pipeline(dve, step, last)


_INS = ['x', 'L0_tok_W', 'L0_tok_b', 'L0_tok_pos_embed', 'L0_attn_w_qkv', 'L0_attn_b_qkv', 'L0_attn_w_proj',
        'L0_attn_b_proj', 'L0_ffn_gate_w', 'L0_ffn_gate_b', 'L0_ffn_w1', 'L0_ffn_w2', 'L0_ffn_w3']
_OUTS = [((4, 1024, 64), 'float32')]


def kernel(**inputs):
    import numpy as _np
    import concourse.bacc as _bacc
    from concourse import mybir as _mybir
    from concourse.bass_utils import run_bass_kernel_spmd as _run

    nc = _bacc.Bacc("TRN2", target_bir_lowering=False, num_devices=1)
    arrays, args = {}, []
    for name in _INS:
        a = _np.ascontiguousarray(inputs[name])
        arrays[f"in_{name}_dram"] = a
        args.append(nc.dram_tensor(f"in_{name}_dram", a.shape, _mybir.dt.from_np(a.dtype), kind="ExternalInput").ap())
    for i, (shape, dtype) in enumerate(_OUTS):
        dt = _mybir.dt.from_np(_np.dtype(dtype))
        args.append(nc.dram_tensor(f"out_{i}_dram", shape, dt, kind="ExternalOutput").ap())
    vit_tower(nc, *args)
    r = _run(nc, [arrays], core_ids=[0])
    return r.results[0]["out_0_dram"]
```

```python
import math
from contextlib import ExitStack

import concourse.bass as bass
from concourse import mybir

ALU = mybir.AluOpType
ACT = mybir.ActivationFunctionType
AX_X = mybir.AxisListType.X
F32 = mybir.dt.float32
F32R = mybir.dt.float32r
BF16 = mybir.dt.bfloat16
I32 = mybir.dt.int32
U32 = mybir.dt.uint32

SLOTS = 32
SCORE_AT = (0, 1, 2, 4)
TURN_AT = 9
PV_AT = 11
EPS = 1e-5
MASKED = -1e30


def vit_tower(nc, x, tok_W, tok_b, pos_embed, w_qkv, b_qkv, w_proj, b_proj, gate_w, gate_b, w1, w2, w3, out):
    IMAGES, _, MELS, FRAMES = x.shape
    E = tok_W.shape[0]
    PATCH = 8
    ROWS, COLS = MELS // PATCH, FRAMES // PATCH // 2
    CHUNKS = 2 * IMAGES
    T = ROWS * COLS
    TILES = T // 128
    H, DH, K = 8, E // 8, 31
    G = T // 32
    SPAN = 32 + K - 1
    SCALE = float(DH) ** -0.5
    X, HID = gate_w.shape[1], w1.shape[2]
    PAIRS = X // 2
    PARTS = 3 * X

    def span_start(j):
        return min(max(32 * j - K // 2, 0), T - SPAN)

    with ExitStack() as ctx:
        def sb(name, shape, dt=F32):
            return ctx.enter_context(nc.sbuf_tensor(name, shape, dt))

        def bank(name):
            return ctx.enter_context(nc.psum_tensor(name, [128, 512], F32))

        def sem(name):
            return ctx.enter_context(nc.semaphore(name))

        ident = sb("ident", [128, 128])
        ident_bf = sb("ident_bf", [128, 128], BF16)
        fold = sb("fold", [128, E])
        mask = sb("mask", [128, 3, H, SPAN], BF16)
        band = sb("band", [128, 3, SPAN])
        spread = sb("spread", [128, PAIRS, 2, 64], BF16)
        iota_x = sb("iota_x", [128, X])
        tokW = sb("tokW", [E, 64])
        tokWT = sb("tokWT", [65, E])
        pos = sb("pos", [128, TILES, 2, E])
        Wqkv = sb("Wqkv", [65, 3 * E])
        Wproj = sb("Wproj", [65, E])
        gate = sb("gate", [128, X])
        gate_bias = sb("gate_bias", [128, X])
        w12 = sb("w12", [128, 2, X, HID])
        w_hi = sb("w_hi", [128, 2, X, HID], F32R)
        w_lo = sb("w_lo", [128, 2, X, HID], F32R)
        w3s = sb("w3s", [HID, X, E])

        x_stage = sb("x_stage", [128, FRAMES])
        by_frame = sb("by_frame", [COLS, 128, PATCH])
        patchT = sb("patchT", [65, T])
        tokens = sb("tokens", [128, 2, TILES, E])
        xn1 = sb("xn1", [128, TILES, E])
        xn1T = sb("xn1T", [65, T])
        qT = sb("qT", [128, T])
        kT = sb("kT", [128, T])
        k_diag = sb("k_diag", [128, H, T])
        v_span = sb("v_span", [128, 2, G, H // 2, 2 * (DH + 1)])
        smax = sb("smax", [128, TILES, H])
        probs = sb("probs", [128, TILES, H, 64])
        probsT = sb("probsT", [128, 2, H // 2, 128])
        inv_sum = sb("inv_sum", [128, TILES, H])
        attn = sb("attn", [128, TILES, E])
        attnT = sb("attnT", [65, T])
        resid = sb("resid", [128, 2, TILES, E])
        xn2 = sb("xn2", [128, TILES, E])
        xn2_parts = sb("xn2_parts", [128, TILES, 2 * E], F32R)
        x2T = sb("x2T", [128, 2, T], F32R)
        logits = sb("logits", [128, TILES, X])
        top = sb("top", [128, TILES, 8])
        top_at = sb("top_at", [128, TILES, 8], U32)
        top_idx = sb("top_idx", [128, TILES, 2])
        top_diff = sb("top_diff", [128, TILES, 2])
        top_exp = sb("top_exp", [128, TILES, 2])
        e_base = sb("e_base", [128, TILES, 2])
        top_sum = sb("top_sum", [128, TILES])
        top_inv = sb("top_inv", [128, TILES])
        top_w = sb("top_w", [128, TILES, 2])
        hot = sb("hot", [128, 2, TILES, X])
        hot_w = sb("hot_w", [128, 2, TILES, X])
        disp = sb("disp", [128, 2, TILES, X])
        disp_parts = sb("disp_parts", [128, TILES, PARTS], BF16)
        dispT = sb("dispT", [128, T], BF16)
        ln = [{"stats": sb(f"stats{n}", [128, TILES, 6]), "mv": sb(f"mv{n}", [128, TILES, 2]),
               "var": sb(f"var{n}", [128, TILES]), "rstd": sb(f"rstd{n}", [128, TILES])} for n in (1, 2)]
        neg_half = sb("neg_half", [128, TILES])
        silu = sb("silu", [128, 2, T])
        hidden = sb("hidden", [128, 4, T])
        weight = sb("weight", [128, 2, T])
        y_w = sb("y_w", [128, 2, T])
        y_sum = sb("y_sum", [128, T])
        result = sb("result", [128, 2, TILES, E])

        b_h1, b_h2, b_y = [bank("b_h1a"), bank("b_h1b")], bank("b_h2"), bank("b_y")
        b_s, b_m = bank("b_s"), bank("b_m")
        b_p = [bank("b_p0"), bank("b_p1")]

        c_zero, c_tri, c_mask, c_band = sem("c_zero"), sem("c_tri"), sem("c_mask"), sem("c_band")
        c_ident, c_masks, c_rows = sem("c_ident"), sem("c_masks"), sem("c_rows")
        pe_apart, dve_apart, pool_apart = sem("pe_apart"), sem("dve_apart"), sem("pool_apart")
        d_tok, d_attn, d_ffn = sem("d_tok"), sem("d_attn"), sem("d_ffn")
        w_turned, w_copied = sem("w_turned"), sem("w_copied")
        hi_split, lo_split = sem("hi_split"), sem("lo_split")
        x_loaded, x_turned = sem("x_loaded"), sem("x_turned")
        frames_copied, patch_turned, patch_copied = sem("frames_copied"), sem("patch_turned"), sem("patch_copied")
        embedded, tokens_made = sem("embedded"), sem("tokens_made")
        ln_dve = [sem("ln1_dve"), sem("ln2_dve")]
        ln_rstd = [sem("ln1_rstd"), sem("ln2_rstd")]
        xn1_made, xn1_turned, xn1_copied = sem("xn1_made"), sem("xn1_turned"), sem("xn1_copied")
        qk_made, v_made, q_copied, k_copied, v_copied = (
            sem("qk_made"), sem("v_made"), sem("q_copied"), sem("k_copied"), sem("v_copied"))
        k_spread = sem("k_spread")
        scored, maxed, centred = sem("scored"), sem("maxed"), sem("centred")
        exped = sem("exped")
        p_turned, p_copied, pv_done = sem("p_turned"), sem("p_copied"), sem("pv_done")
        inverted, attn_made, attn_turned, attn_copied = (
            sem("inverted"), sem("attn_made"), sem("attn_turned"), sem("attn_copied"))
        projected, resid_made = sem("projected"), sem("resid_made")
        xn2_made, hi_made, lo_made = sem("xn2_made"), sem("hi_made"), sem("lo_made")
        x2_turned, x2_copied = sem("x2_turned"), sem("x2_copied")
        gated, biased, topped, top_found, idx_made, diffed, top_exped = (
            sem("gated"), sem("biased"), sem("topped"), sem("top_found"), sem("idx_made"), sem("diffed"),
            sem("top_exped"))
        idx_cast = sem("idx_cast")
        summed2, inverted2, weighed = sem("summed2"), sem("inverted2"), sem("weighed")
        routed = sem("routed")
        disp_turned, disp_copied = sem("disp_turned"), sem("disp_copied")
        h1_done, h2_done, silu_done, hid_done = sem("h1_done"), sem("h2_done"), sem("silu_done"), sem("hid_done")
        y_done, w_done, w_held, yw_done = sem("y_done"), sem("w_done"), sem("w_held"), sem("yw_done")
        summed = sem("summed")
        folded, result_made = sem("folded"), sem("result_made")
        stored = [sem("stored0"), sem("stored1")]
        ROUTE, LNS = 7, 3

        def cid(chunk):
            return 2 * chunk[0] + chunk[1]

        def wait(eng, s, n):
            if not isinstance(n, int) or n > 0:
                eng.wait_ge(s, n)

        apart = {nc.tensor.engine: pe_apart, nc.vector.engine: dve_apart, nc.gpsimd.engine: pool_apart}

        def wait_apart(eng, s, n):
            wait(eng, s, n)
            if not isinstance(n, int):
                eng.sem_inc(apart[eng.engine], 1)

        def run_pipeline(eng, step, last):
            step(embed=(0, 0))
            step(embed=(0, 1), qkv=(0, 0))
            step(embed=(1, 0), qkv=(0, 1), attend=(0, 0))
            step(embed=(1, 1), qkv=(1, 0), attend=(0, 1), experts=(0, 0))
            with eng.Fori(1, IMAGES) as b:
                step(embed=(b + 1, 0), qkv=(b, 1), attend=(b, 0), experts=(b - 1, 1), finish=(b - 1, 0))
                step(embed=(b + 1, 1), qkv=(b + 1, 0), attend=(b, 1), experts=(b, 0), finish=(b - 1, 1))
            step(experts=(IMAGES - 1, 1), finish=(IMAGES - 1, 0))
            last((IMAGES - 1, 1))

        block = ctx.enter_context(nc.Block())

        @block.sync
        def _(sp):
            sp.dma_start(x_stage[:], x[0, 0]).then_inc(x_loaded, 16)
            sp.dma_start(pos[:], pos_embed[0].rearrange("(t p g) e -> p t g e", t=TILES, g=2)).then_inc(d_tok, 16)
            for half in range(2):
                sp.dma_start(gate[64 * half:64 * half + 64, :], gate_w).then_inc(d_attn, 16)
            sp.dma_start(gate_bias[:], gate_b.partition_broadcast(128)).then_inc(d_attn, 16)
            for n in range(2):
                for half in range(2):
                    sp.dma_start(w12[64 * half:64 * half + 64, n],
                                 (w1, w2)[n].rearrange("e d h -> d e h")).then_inc(d_ffn, 16)
            sp.dma_start(w3s[:], w3.rearrange("e h o -> h e o")).then_inc(d_ffn, 16)

            def load_image(b):
                sp.wait_ge(x_turned, 2 * b)
                sp.dma_start(x_stage[:], x[b, 0]).then_inc(x_loaded, 16)

            def spread_keys(chunk):
                sp.wait_ge(k_copied, cid(chunk) + 1)
                for h in range(H):
                    sp.dma_start(k_diag[DH * h:DH * h + DH, h, :],
                                 kT[64 + DH * h:64 + DH * h + DH, :]).then_inc(k_spread, 16)

            def store(chunk):
                b, g = chunk
                sp.wait_ge(result_made, cid(chunk) + 1)
                sp.dma_start(out[b].rearrange("(t p g) e -> g p t e", t=TILES, g=2)[g],
                             result[:, g]).then_inc(stored[g], 16)

            sp.wait_ge(c_rows, 3)
            spread_keys((0, 0))
            load_image(1)
            spread_keys((0, 1))
            spread_keys((1, 0))
            with sp.Fori(1, IMAGES - 1) as b:
                store((b - 1, 0))
                load_image(b + 1)
                spread_keys((b, 1))
                store((b - 1, 1))
                spread_keys((b + 1, 0))
            store((IMAGES - 2, 0))
            sp.wait_ge(x_turned, 2 * IMAGES)
            sp.dma_start(x_stage[:], x[0, 0]).then_inc(x_loaded, 16)
            spread_keys((IMAGES - 1, 1))
            store((IMAGES - 2, 1))
            spread_keys((IMAGES, 0))
            store((IMAGES - 1, 0))
            store((IMAGES - 1, 1))
            for g in range(2):
                sp.wait_ge(stored[g], 16 * IMAGES)
            sp.wait_ge(x_loaded, 16 * (IMAGES + 1))
            sp.wait_ge(k_spread, 16 * H * (CHUNKS + 1))

        @block.gpsimd
        def _(pool):
            pool.memset(ident[:], 0.0).then_inc(c_zero, 1)
            pool.wait_ge(c_zero, 1)
            pool.affine_select(out=ident[:], in_=ident[:], compare_op=ALU.not_equal, fill=1.0, base=0,
                               pattern=[[-1, 128]], channel_multiplier=1).then_inc(c_ident, 1)
            pool.memset(neg_half[:], -0.5)
            pool.memset(e_base[:], math.e).then_inc(c_zero, 1)
            pool.wait_ge(c_ident, 1)
            pool.tensor_copy(ident_bf[:], ident[:]).then_inc(c_tri, 1)

            steps = [0]

            def keep(row0, tiles, base, mult, step, fill):
                pool.wait_ge(c_mask, steps[0])
                part = band[row0:row0 + 32, tiles]
                pool.affine_select(out=part, in_=part, compare_op=ALU.is_ge, fill=fill, base=base,
                                   pattern=[[0, tiles.stop - tiles.start], [step, SPAN]],
                                   channel_multiplier=mult).then_inc(c_mask, 1)
                steps[0] += 1

            def step_done(ins):
                ins.then_inc(c_mask, 1)
                steps[0] += 1

            step_done(pool.memset(band[:], 0.0))
            for row0, tiles in ((0, slice(1, 3)), (32, slice(0, 3)), (64, slice(0, 3)), (96, slice(0, 2))):
                keep(row0, tiles, 0, -1, 1, MASKED)
                keep(row0, tiles, K - 1, 1, -1, MASKED)
            keep(0, slice(0, 1), K - 1, 0, -1, MASKED)
            keep(0, slice(0, 1), -(K // 2 + 1), -1, 1, 0.0)
            keep(0, slice(0, 1), K // 2, -1, 1, MASKED)
            keep(96, slice(2, 3), -(SPAN - K), 0, 1, MASKED)
            keep(96, slice(2, 3), K // 2 - 1, 1, -1, 0.0)
            keep(96, slice(2, 3), K // 2 + K - 1, 1, -1, MASKED)
            pool.wait_ge(c_tri, 1)
            pool.wait_ge(c_mask, steps[0])
            pool.memset(fold[:], 0.0).then_inc(c_band, 1)

            def make_fold_and_spread():
                pool.memset(spread[:], 0.0).then_inc(c_zero, 1)
                pool.wait_ge(c_band, 1)
                for k in range(2):
                    pool.affine_select(out=fold[:], in_=fold[:], compare_op=ALU.not_equal, fill=1.0, base=-E * k,
                                       pattern=[[-1, E]], channel_multiplier=1).then_inc(c_tri, 1)
                    pool.wait_ge(c_tri, k + 2)
                pool.wait_ge(c_zero, 3)
                for part in range(3):
                    step_done(pool.affine_select(out=spread[:], in_=spread[:], compare_op=ALU.not_equal, fill=1.0,
                                                 base=-X * part, pattern=[[-2, PAIRS], [-1, 2], [0, 64]],
                                                 channel_multiplier=1))
                    pool.wait_ge(c_mask, steps[0])
                pool.iota(iota_x[:], pattern=[[1, X]], base=0, channel_multiplier=0,
                          allow_small_or_imprecise_dtypes=True).then_inc(c_band, 1)

            def rsqrt(n, c):
                pool.wait_ge(ln_dve[n], LNS * c + 3)
                pool.tensor_tensor(ln[n]["rstd"][:], ln[n]["var"][:], neg_half[:], ALU.pow).then_inc(ln_rstd[n], 1)

            def exp_top(c):
                pool.wait_ge(diffed, c + 1)
                pool.tensor_tensor(top_exp[:], e_base[:], top_diff[:], ALU.pow).then_inc(top_exped, 1)

            def route(c):
                pool.wait_ge(idx_made, c + 1)
                pool.wait_ge(weighed, c + 1)
                for k in range(2):
                    pool.tensor_tensor(hot_w[:, k], hot[:, k],
                                       top_w[:, :, k].unsqueeze(2).to_broadcast([128, TILES, X]),
                                       ALU.mult).then_inc(routed, 1)
                pool.wait_ge(routed, ROUTE * c + 2)
                pool.tensor_tensor(disp[:, 0], hot_w[:, 0], hot_w[:, 1], ALU.add).then_inc(routed, 1)
                wait(pool, disp_turned, c)
                for k in range(2):
                    part = disp_parts[:, :, X * k:X * k + X]
                    wait_apart(pool, routed, ROUTE * c + 3 + 2 * k)
                    pool.tensor_copy(part, disp[:, k]).then_inc(routed, 1)
                    pool.wait_ge(routed, ROUTE * c + 4 + 2 * k)
                    rest = disp[:, 1] if k == 0 else disp_parts[:, :, 2 * X:3 * X]
                    pool.tensor_tensor(rest, disp[:, k], part, ALU.subtract).then_inc(routed, 1)

            def add_pair(c, q):
                pool.wait_ge(yw_done, PAIRS * c + q + 1)
                if q == 1:
                    wait(pool, folded, c)
                    pool.tensor_tensor(y_sum[:], y_w[:, 0], y_w[:, 1], ALU.add).then_inc(summed, 1)
                else:
                    pool.wait_ge(summed, (PAIRS - 1) * c + q - 1)
                    pool.tensor_tensor(y_sum[:], y_sum[:], y_w[:, q % 2], ALU.add).then_inc(summed, 1)

            def step(embed=None, qkv=None, attend=None, experts=None, finish=None):
                for s in range(SLOTS):
                    if s == 0 and attend is not None and experts is None:
                        make_fold_and_spread()
                    if s == 19 and attend is not None:
                        rsqrt(1, cid(attend))
                    if s == 20 and embed is not None:
                        rsqrt(0, cid(embed))
                    if s == 25 and attend is not None:
                        exp_top(cid(attend))
                    if s == 1 and finish is not None:
                        add_pair(cid(finish), PAIRS - 1)
                    if experts is not None and s % 4 == 1 and s > 5:
                        add_pair(cid(experts), (s - 5) // 4)
                    if s == 28 and attend is not None:
                        route(cid(attend))

            run_pipeline(pool, step, lambda chunk: add_pair(cid(chunk), PAIRS - 1))

        @block.tensor
        def _(pe):
            pe.wait_ge(c_ident, 1)
            pe.wait_ge(d_tok, 48)
            pe.transpose(b_s[0:64, 0:E], tokW[:], ident[0:E, 0:E]).then_inc(w_turned, 1)

            def turn_frames(chunk):
                b, g = chunk
                c = cid(chunk)
                pe.wait_ge(x_loaded, 16 * b + 16)
                if isinstance(c, int) and c == 1:
                    pe.wait_ge(tokens_made, c)
                wait(pe, p_copied, TILES * (c - 1))
                cols = x_stage[:].rearrange("r (f g j) -> r g j f", g=2, j=PATCH)[:, g]
                for j in range(PATCH):
                    ins = pe.transpose(b_p[j // 4][0:COLS, 128 * (j % 4):128 * (j % 4) + 128], cols[:, j],
                                       ident[:])
                ins.then_inc(x_turned, 1)

            def turn_patches(chunk):
                c = cid(chunk)
                wait_apart(pe, frames_copied, c + 1)
                for m in range(ROWS):
                    ins = pe.transpose(b_p[0][0:64, COLS * m:COLS * m + COLS],
                                       by_frame[:, PATCH * m:PATCH * m + PATCH].rearrange("f i j -> f (i j)"),
                                       ident[0:COLS, 0:COLS])
                ins.then_inc(patch_turned, 1)

            def embed_patches(chunk):
                c = cid(chunk)
                if isinstance(c, int) and c == 0:
                    pe.wait_ge(w_copied, 1)
                    pe.wait_ge(c_rows, 1)
                pe.wait_ge(patch_copied, c + 1)
                for t in range(TILES):
                    ins = pe.matmul(b_p[1][:, E * t:E * t + E], patchT[:, 128 * t:128 * t + 128], tokWT[:],
                                    start=True, stop=True)
                ins.then_inc(embedded, 1)

            def turn_xn1(chunk):
                wait(pe, centred, TILES * cid(chunk))
                wait_apart(pe, xn1_made, cid(chunk) + 1)
                for t in range(TILES):
                    ins = pe.transpose(b_s[0:E, 128 * t:128 * t + 128], xn1[:, t], ident[:])
                ins.then_inc(xn1_turned, 1)

            def make_qk(chunk):
                c = cid(chunk)
                if isinstance(c, int) and c == 0:
                    pe.wait_ge(d_attn, 16 * 7)
                pe.wait_ge(xn1_copied, c + 1)
                pe.matmul(b_s[:], Wqkv[:, 0:2 * E], xn1T[:], start=True, stop=True).then_inc(qk_made, 1)

            def make_v(chunk):
                c = cid(chunk)
                pe.wait_ge(q_copied, c + 1)
                pe.wait_ge(k_copied, c + 1)
                Wv = Wqkv[:, 2 * E:3 * E].rearrange("k (p r d) -> k r p d", r=2, d=DH)
                for j in range(G):
                    k0 = span_start(j)
                    for r in range(2):
                        ins = pe.matmul(b_s[64 * r:64 * r + SPAN, E // 2 * j:E // 2 * (j + 1)],
                                        xn1T[:, k0:k0 + SPAN], Wv[:, r], start=True, stop=True)
                ins.then_inc(v_made, 1)

            def score(chunk, t):
                c = cid(chunk)
                dst = (b_s, b_p[0], b_p[1], b_s)[t][:, 0:H * SPAN]
                if t == 0:
                    if isinstance(c, int) and c == 0:
                        pe.wait_ge(c_masks, 1)
                        pe.wait_ge(c_rows, 3)
                    pe.wait_ge(k_spread, 16 * H * (c + 1))
                    pe.wait_ge(q_copied, c + 1)
                    pe.wait_ge(v_copied, c + 1)
                    wait(pe, x2_copied, c)
                if t == 1:
                    pe.wait_ge(patch_copied, c + 2)
                if t == 2:
                    pe.wait_ge(tokens_made, c + 2)
                if t == 3:
                    pe.wait_ge(centred, TILES * c + 1)
                which = 0 if t == 0 else 2 if t == TILES - 1 else 1
                pe.matmul(dst, ident_bf[:], mask[:, which].rearrange("p h k -> p (h k)"), start=True, stop=False,
                          skip_group_check=True)
                for g in range(4):
                    k0 = span_start(4 * t + g)
                    ins = pe.matmul(dst[32 * g:32 * g + 32, :], qT[:, 128 * t + 32 * g:128 * t + 32 * g + 32],
                                    k_diag[:, :, k0:k0 + SPAN], start=False, stop=True, skip_group_check=True)
                ins.then_inc(scored, 1)

            def turn_probs(chunk, t):
                c = cid(chunk)
                if t == 0:
                    wait_apart(pe, exped, c + 1)
                if t >= 2:
                    wait_apart(pe, p_copied, TILES * c + t - 1)
                for k in range(H // 2):
                    ins = pe.transpose(b_p[t % 2][:, 128 * k:128 * k + 128],
                                       probs[:, t, 2 * k:2 * k + 2].rearrange("p h k -> p (h k)"), ident[:])
                ins.then_inc(p_turned, 1)

            def apply_probs(chunk, t):
                c = cid(chunk)
                pe.wait_ge(p_copied, TILES * c + t + 1)
                if t == 0:
                    wait(pe, disp_copied, c)
                    wait(pe, result_made, c - 1)
                o = b_m[:, 0:TILES * H * (DH + 1)].rearrange("p (t k d) -> p t k d", t=TILES, k=H // 2)
                for k in range(H // 2):
                    for g in range(4):
                        ins = pe.matmul(o[32 * g:32 * g + 32, t, k], probsT[:, t % 2, k, 32 * g:32 * g + 32],
                                        v_span[:, chunk[1], 4 * t + g, k], start=True, stop=True)
                ins.then_inc(pv_done, 1)

            def turn_attn(chunk):
                pe.wait_ge(attn_made, cid(chunk) + 1)
                wait_apart(pe, v_copied, cid(chunk) + 2)
                for t in range(TILES):
                    ins = pe.transpose(b_s[0:E, 128 * t:128 * t + 128], attn[:, t], ident[:])
                ins.then_inc(attn_turned, 1)

            def project(chunk):
                pe.wait_ge(attn_copied, cid(chunk) + 1)
                for t in range(TILES):
                    ins = pe.matmul(b_m[:, E * t:E * t + E], attnT[:, 128 * t:128 * t + 128], Wproj[:],
                                    start=True, stop=True)
                ins.then_inc(projected, 1)

            def turn_x2(chunk):
                pe.wait_ge(hi_made, cid(chunk) + 1)
                pe.wait_ge(lo_made, cid(chunk) + 1)
                for t in range(TILES):
                    ins = pe.transpose(b_s[:, 128 * t:128 * t + 128], xn2_parts[:, t].bitcast(F32), ident[:])
                ins.then_inc(x2_turned, 1)

            def make_logits(chunk):
                b, g = chunk
                pe.wait_ge(x2_copied, cid(chunk) + 1)
                for t in range(TILES):
                    ins = pe.matmul(b_m[:, X * t:X * t + X], x2T[:, g, 128 * t:128 * t + 128].bitcast(F32),
                                    gate[:], start=True, stop=True)
                ins.then_inc(gated, 1)

            def turn_disp(chunk):
                wait_apart(pe, routed, ROUTE * (cid(chunk) + 1))
                dst = b_m[:].bitcast(BF16)
                for t in range(TILES):
                    ins = pe.transpose(dst[0:PARTS, 128 * t:128 * t + 128], disp_parts[:, t], ident_bf[:])
                ins.then_inc(disp_turned, 1)

            def up(chunk, e, n):
                b, g = chunk
                c = cid(chunk)
                if e == 0 and n == 0:
                    pe.wait_ge(x2_copied, c + 1)
                    if isinstance(c, int) and c == 0:
                        pe.wait_ge(hi_split, 2)
                        pe.wait_ge(lo_split, 2)
                if n == 0:
                    dst, made = b_h1[e % 2], h1_done
                    wait(pe, silu_done, X * c + e - 1)
                else:
                    dst, made = b_h2, h2_done
                    wait(pe, hid_done, X * c + e)
                pe.matmul(dst[:], w_hi[:, n, e], x2T[:, g], start=True, stop=False)
                pe.matmul(dst[:], w_lo[:, n, e], x2T[:, g], start=False, stop=True).then_inc(made, 1)

            def down(chunk, q):
                c = cid(chunk)
                pe.wait_ge(hid_done, X * c + 2 * q + 2)
                pe.wait_ge(w_held, PAIRS * c + q + 1)
                for k in range(2):
                    ins = pe.matmul(b_y[64 * k:64 * k + 64, :], w3s[:, 2 * q + k], hidden[:, (2 * q + k) % 4],
                                    start=True, stop=True)
                ins.then_inc(y_done, 1)

            def spread_weights(chunk, q):
                c = cid(chunk)
                if q == 0:
                    pe.wait_ge(disp_copied, c + 1)
                    if isinstance(c, int) and c == 0:
                        pe.wait_ge(c_band, 2)
                wait(pe, yw_done, PAIRS * c + q)
                pe.matmul(b_y[:], spread[:, q].rearrange("p a b -> p (a b)"), dispT[:], start=True,
                          stop=True).then_inc(w_done, 1)

            def fold_pairs(chunk):
                c = cid(chunk)
                pe.wait_ge(summed, (PAIRS - 1) * (c + 1))
                pe.wait_ge(disp_copied, min(c + 2, CHUNKS) if isinstance(c, int) else c + 2)
                for t in range(TILES):
                    ins = pe.matmul(b_m[:, E * t:E * t + E], y_sum[:, 128 * t:128 * t + 128], fold[:],
                                    start=True, stop=True)
                ins.then_inc(folded, 1)

            def step(embed=None, qkv=None, attend=None, experts=None, finish=None):
                for s in range(SLOTS):
                    if experts is not None:
                        if s % 2 == 0:
                            if s // 2 + 1 < X:
                                up(experts, s // 2 + 1, 0)
                            up(experts, s // 2, 1)
                        if s % 4 == 3:
                            spread_weights(experts, (s - 3) // 4)
                        if s % 4 == 1 and s >= 5:
                            down(experts, (s - 5) // 4)
                    if experts is not None and s == 1:
                        turn_disp(experts)
                    if finish is not None:
                        if s == 1:
                            down(finish, PAIRS - 1)
                        if s == 3:
                            fold_pairs(finish)
                    if attend is not None:
                        if s in SCORE_AT:
                            score(attend, SCORE_AT.index(s))
                        if PV_AT <= s < PV_AT + TILES:
                            apply_probs(attend, s - PV_AT)
                        if TURN_AT <= s < TURN_AT + TILES:
                            turn_probs(attend, s - TURN_AT)
                    if qkv is not None:
                        if s == 7:
                            turn_xn1(qkv)
                        if s == 9:
                            make_qk(qkv)
                        if s == 12:
                            make_v(qkv)
                    if attend is not None:
                        if s == 16:
                            turn_attn(attend)
                        if s == 17:
                            project(attend)
                        if s == 22:
                            turn_x2(attend)
                        if s == 24:
                            make_logits(attend)
                        if s == 31:
                            up(attend, 0, 0)
                    if embed is not None:
                        if s == 15:
                            turn_frames(embed)
                        if s == 17:
                            turn_patches(embed)
                        if s == 19:
                            embed_patches(embed)

            def last(chunk):
                down(chunk, PAIRS - 1)
                fold_pairs(chunk)

            run_pipeline(pe, step, last)

        @block.scalar
        def _(act):
            act.dma_start(tokW[:], tok_W).then_inc(d_tok, 16)
            act.dma_start(tokWT[64:65, :], tok_b.rearrange("(a e) -> a e", a=1)).then_inc(d_tok, 16)
            act.dma_start(Wqkv[0:E, :], w_qkv).then_inc(d_attn, 16)
            act.dma_start(Wqkv[64:65, :], b_qkv.rearrange("(a e) -> a e", a=1)).then_inc(d_attn, 16)
            act.dma_start(Wproj[0:E, :], w_proj).then_inc(d_attn, 16)
            act.dma_start(Wproj[64:65, :], b_proj.rearrange("(a e) -> a e", a=1)).then_inc(d_attn, 16)
            act.wait_ge(w_turned, 1)
            nc.scalar.copy(tokWT[0:64, :], b_s[0:64, 0:E]).then_inc(w_copied, 1)

            def copy_frames(chunk):
                c = cid(chunk)
                act.wait_ge(x_turned, c + 1)
                wait(act, patch_turned, c)
                for k in range(2):
                    ins = nc.scalar.copy(by_frame[:, :, 4 * k:4 * k + 4].rearrange("f r j -> f j r"),
                                         b_p[k][0:COLS, :].rearrange("f (j r) -> f j r", j=4))
                ins.then_inc(frames_copied, 1)

            def copy_patches(chunk):
                c = cid(chunk)
                act.wait_ge(patch_turned, c + 1)
                wait(act, embedded, c)
                nc.scalar.copy(patchT[0:64, :], b_p[0][0:64, :]).then_inc(patch_copied, 1)

            def copy_qk(chunk):
                c = cid(chunk)
                act.wait_ge(qk_made, c + 1)
                if isinstance(c, int) and c == 0:
                    act.wait_ge(c_rows, 3)
                wait(act, k_spread, 16 * H * c)
                nc.scalar.copy(kT[64:128, :], b_s[64:128, :]).then_inc(k_copied, 1)
                nc.scalar.mul(qT[0:64, :], b_s[0:64, :], SCALE).then_inc(q_copied, 1)

            def exp_scores(chunk):
                c = cid(chunk)
                act.wait_ge(centred, TILES * (c + 1))
                spans = probs[:].rearrange("p t h k -> p (t h) k")[:, :, 0:SPAN]
                nc.scalar.activation(spans, spans, ACT.Exp).then_inc(exped, 1)

            def copy_probs(chunk, t):
                n = TILES * cid(chunk) + t
                act.wait_ge(p_turned, n + 1)
                wait(act, pv_done, n - 1)
                nc.scalar.copy(probsT[:, t % 2].rearrange("p k q -> p (k q)"), b_p[t % 2][:]).then_inc(p_copied, 1)

            def copy_attn(chunk):
                act.wait_ge(attn_turned, cid(chunk) + 1)
                nc.scalar.copy(attnT[0:E, :], b_s[0:E, :]).then_inc(attn_copied, 1)

            def copy_x2(chunk):
                b, g = chunk
                act.wait_ge(x2_turned, cid(chunk) + 1)
                nc.scalar.copy(x2T[:, g], b_s[:]).then_inc(x2_copied, 1)

            def copy_disp(chunk):
                c = cid(chunk)
                act.wait_ge(disp_turned, c + 1)
                wait(act, w_done, PAIRS * c)
                nc.scalar.copy(dispT[0:PARTS, :], b_m[:].bitcast(BF16)[0:PARTS, 0:T]).then_inc(disp_copied, 1)

            def silu_up(chunk, e):
                n = X * cid(chunk) + e
                act.wait_ge(h1_done, n + 1)
                wait(act, hid_done, n - 1)
                nc.scalar.activation(silu[:, e % 2], b_h1[e % 2][:], ACT.Silu).then_inc(silu_done, 1)

            def hold_weights(chunk, q):
                n = PAIRS * cid(chunk) + q
                act.wait_ge(w_done, n + 1)
                wait(act, yw_done, n - 1)
                nc.scalar.copy(weight[:, q % 2], b_y[:]).then_inc(w_held, 1)

            def step(embed=None, qkv=None, attend=None, experts=None, finish=None):
                for s in range(SLOTS):
                    if experts is not None:
                        if s % 2 == 0 and s // 2 + 1 < X:
                            silu_up(experts, s // 2 + 1)
                        if s % 4 == 3:
                            hold_weights(experts, (s - 3) // 4)
                    if experts is not None and s == 1:
                        copy_disp(experts)
                    if attend is not None:
                        if s == SCORE_AT[-1] + 1:
                            exp_scores(attend)
                        if TURN_AT <= s < TURN_AT + TILES:
                            copy_probs(attend, s - TURN_AT)
                        if s == 16:
                            copy_attn(attend)
                        if s == 22:
                            copy_x2(attend)
                        if s == 31:
                            silu_up(attend, 0)
                    if qkv is not None and s == 9:
                        copy_qk(qkv)
                    if embed is not None:
                        if s == 15:
                            copy_frames(embed)
                        if s == 17:
                            copy_patches(embed)
                if attend is None and qkv is not None:
                    act.wait_ge(d_ffn, 16 * 5)
                    for n in range(2):
                        nc.scalar.copy(w_hi[:, n].rearrange("p e h -> p (e h)"),
                                       w12[:, n].rearrange("p e h -> p (e h)")).then_inc(hi_split, 1)

            run_pipeline(act, step, lambda chunk: None)

        @block.vector
        def _(dve):
            nc.vector.memset(patchT[64:65, :], 1.0)
            nc.vector.memset(xn1T[64:65, :], 1.0)
            nc.vector.memset(attnT[64:65, :], 1.0).then_inc(c_rows, 1)
            nc.vector.memset(v_span[:], 0.0).then_inc(c_rows, 1)
            nc.vector.memset(qT[64:128, :], 0.0)
            nc.vector.memset(dispT[:], 0.0)
            nc.vector.memset(probs[:, :, :, SPAN:64], 0.0)
            dve.wait_ge(c_rows, 2)
            for r in range(2):
                nc.vector.memset(v_span[64 * r:64 * r + 64, :, :, :, (DH + 1) * r + DH], 1.0)
            nc.vector.memset(k_diag[:], 0.0).then_inc(c_rows, 1)
            dve.wait_ge(c_rows, 3)
            dve.wait_ge(d_tok, 48)

            def make_masks():
                dve.wait_ge(c_band, 1)
                for n in range(3):
                    ins = nc.vector.tensor_copy(mask[:, n], band[:, n].unsqueeze(1).to_broadcast([128, H, SPAN]))
                ins.then_inc(c_masks, 1)

            def stats(n, src, c):
                d, s = ln[n], ln_dve[n]
                for t in range(TILES):
                    ins = nc.vector.bn_stats(d["stats"][:, t], src[:, t])
                ins.then_inc(s, 1)
                wait_apart(dve, s, LNS * c + 1)
                for t in range(TILES):
                    ins = nc.vector.bn_aggr(d["mv"][:, t], d["stats"][:, t])
                ins.then_inc(s, 1)
                dve.wait_ge(s, LNS * c + 2)
                nc.vector.tensor_scalar(d["var"][:], d["mv"][:, :, 1], EPS, None, ALU.add).then_inc(s, 1)

            def normalise(n, dst, src, c, made):
                d = ln[n]
                dve.wait_ge(ln_rstd[n], c + 1)
                for t in range(TILES):
                    ins = nc.vector.tensor_scalar(dst[:, t], src[:, t], d["mv"][:, t, 0:1],
                                                  d["rstd"][:, t:t + 1], ALU.subtract, ALU.mult)
                ins.then_inc(made, 1)

            def make_tokens(chunk):
                b, g = chunk
                c = cid(chunk)
                dve.wait_ge(embedded, c + 1)
                nc.vector.tensor_tensor(tokens[:, g], b_p[1][:, 0:TILES * E].rearrange("p (t e) -> p t e", t=TILES),
                                        pos[:, :, g], ALU.add).then_inc(tokens_made, 1)
                dve.wait_ge(tokens_made, c + 1)
                stats(0, tokens[:, g], c)

            def normalise1(chunk):
                b, g = chunk
                c = cid(chunk)
                wait(dve, xn1_turned, c)
                normalise(0, xn1, tokens[:, g], c, xn1_made)

            def copy_xn1(chunk):
                c = cid(chunk)
                wait(dve, v_made, c)
                dve.wait_ge(xn1_turned, c + 1)
                nc.vector.tensor_copy(xn1T[0:E, :], b_s[0:E, :]).then_inc(xn1_copied, 1)

            def copy_v(chunk):
                c = cid(chunk)
                wait(dve, pv_done, TILES * (c - 1))
                dve.wait_ge(v_made, c + 1)
                for r in range(2):
                    rows = slice(64 * r, 64 * r + SPAN)
                    ins = nc.vector.tensor_copy(
                        v_span[rows, chunk[1], :, :, (DH + 1) * r:(DH + 1) * r + DH],
                        b_s[rows, :].rearrange("p (j k d) -> p j k d", k=H // 2, d=DH))
                ins.then_inc(v_copied, 1)

            def centre(chunk, t):
                n = TILES * cid(chunk) + t
                src = (b_s, b_p[0], b_p[1], b_s)[t][:, 0:H * SPAN].rearrange("p (h k) -> p h k", h=H)
                dve.wait_ge(scored, n + 1)
                nc.vector.tensor_reduce(smax[:, t], src, AX_X, ALU.max).then_inc(maxed, 1)
                if t == 0:
                    wait(dve, p_turned, n)
                dve.wait_ge(maxed, n + 1)
                nc.vector.tensor_tensor(probs[:, t, :, 0:SPAN], src,
                                        smax[:, t].unsqueeze(2).to_broadcast([128, H, SPAN]),
                                        ALU.subtract).then_inc(centred, 1)

            def divide(chunk):
                c = cid(chunk)
                dve.wait_ge(pv_done, TILES * (c + 1))
                o = b_m[:, 0:TILES * H * (DH + 1)].rearrange("p (th d) -> p th d", d=DH + 1)
                nc.vector.reciprocal(inv_sum[:].rearrange("p t h -> p (t h)"), o[:, :, DH]).then_inc(inverted, 1)
                dve.wait_ge(inverted, c + 1)
                nc.vector.tensor_tensor(
                    attn[:].rearrange("p t (h d) -> p (t h) d", d=DH), o[:, :, 0:DH],
                    inv_sum[:].rearrange("p t h -> p (t h)").unsqueeze(2).to_broadcast([128, TILES * H, DH]),
                    ALU.mult).then_inc(attn_made, 1)

            def add_attention(chunk):
                b, g = chunk
                c = cid(chunk)
                dve.wait_ge(projected, c + 1)
                nc.vector.tensor_tensor(resid[:, g], b_m[:, 0:TILES * E].rearrange("p (t e) -> p t e", t=TILES),
                                        tokens[:, g], ALU.add).then_inc(resid_made, 1)
                dve.wait_ge(resid_made, c + 1)
                stats(1, resid[:, g], c)

            def normalise2(chunk):
                b, g = chunk
                c = cid(chunk)
                normalise(1, xn2, resid[:, g], c, xn2_made)
                dve.wait_ge(xn2_made, c + 1)
                nc.vector.tensor_copy(xn2_parts[:, :, 0:E], xn2[:]).then_inc(hi_made, 1)
                dve.wait_ge(hi_made, c + 1)
                nc.vector.tensor_tensor(xn2_parts[:, :, E:2 * E], xn2[:], xn2_parts[:, :, 0:E].bitcast(F32),
                                        ALU.subtract).then_inc(lo_made, 1)

            def pick_top(chunk):
                c = cid(chunk)
                dve.wait_ge(gated, c + 1)
                if isinstance(c, int) and c == 0:
                    dve.wait_ge(d_attn, 16 * 7)
                nc.vector.tensor_tensor(
                    logits[:], b_m[:, 0:TILES * X].rearrange("p (t x) -> p t x", t=TILES),
                    gate_bias[:].unsqueeze(1).to_broadcast([128, TILES, X]), ALU.add).then_inc(biased, 1)
                wait_apart(dve, biased, c + 1)
                for t in range(TILES):
                    ins = nc.vector.max(top[:, t], logits[:, t])
                ins.then_inc(topped, 1)
                dve.wait_ge(topped, c + 1)
                nc.vector.tensor_tensor(top_diff[:], top[:, :, 0:2],
                                        top[:, :, 0:1].to_broadcast([128, TILES, 2]),
                                        ALU.subtract).then_inc(diffed, 1)
                for t in range(TILES):
                    ins = nc.vector.max_index(top_at[:, t], top[:, t], logits[:, t])
                ins.then_inc(top_found, 1)
                dve.wait_ge(top_found, c + 1)
                nc.vector.tensor_copy(top_idx[:], top_at[:, :, 0:2]).then_inc(idx_cast, 1)
                dve.wait_ge(idx_cast, c + 1)
                if isinstance(c, int) and c == 0:
                    dve.wait_ge(c_band, 2)
                wait(dve, routed, ROUTE * c)
                for k in range(2):
                    ins = nc.vector.tensor_tensor(
                        hot[:, k], iota_x[:].unsqueeze(1).to_broadcast([128, TILES, X]),
                        top_idx[:, :, k].unsqueeze(2).to_broadcast([128, TILES, X]), ALU.is_equal)
                ins.then_inc(idx_made, 1)

            def weigh_top(chunk):
                c = cid(chunk)
                dve.wait_ge(top_exped, c + 1)
                nc.vector.tensor_tensor(top_sum[:], top_exp[:, :, 0], top_exp[:, :, 1], ALU.add).then_inc(summed2, 1)
                dve.wait_ge(summed2, c + 1)
                nc.vector.reciprocal(top_inv[:], top_sum[:]).then_inc(inverted2, 1)
                dve.wait_ge(inverted2, c + 1)
                nc.vector.tensor_tensor(top_w[:], top_exp[:],
                                        top_inv[:].unsqueeze(2).to_broadcast([128, TILES, 2]),
                                        ALU.mult).then_inc(weighed, 1)

            def gate_hidden(chunk, e):
                n = X * cid(chunk) + e
                dve.wait_ge(silu_done, n + 1)
                dve.wait_ge(h2_done, n + 1)
                wait(dve, y_done, PAIRS * cid(chunk) + e // 2 - 1)
                nc.vector.tensor_tensor(hidden[:, e % 4], silu[:, e % 2], b_h2[:], ALU.mult).then_inc(hid_done, 1)

            def weigh_pair(chunk, q):
                c = cid(chunk)
                n = PAIRS * c + q
                dve.wait_ge(y_done, n + 1)
                dve.wait_ge(w_held, n + 1)
                wait(dve, summed, (PAIRS - 1) * c + (q - 1 if q < 2 else max(q - 2, 1)))
                nc.vector.tensor_tensor(y_w[:, q % 2], b_y[:], weight[:, q % 2], ALU.mult).then_inc(yw_done, 1)

            def make_result(chunk):
                b, g = chunk
                c = cid(chunk)
                dve.wait_ge(folded, c + 1)
                wait(dve, stored[g], 16 * b)
                nc.vector.tensor_tensor(result[:, g], b_m[:, 0:TILES * E].rearrange("p (t e) -> p t e", t=TILES),
                                        resid[:, g], ALU.add).then_inc(result_made, 1)

            def step(embed=None, qkv=None, attend=None, experts=None, finish=None):
                for s in range(SLOTS):
                    if finish is not None:
                        if s == 1:
                            weigh_pair(finish, PAIRS - 1)
                        if s == 3:
                            make_result(finish)
                    if experts is not None:
                        if s % 2 == 0:
                            gate_hidden(experts, s // 2)
                        if s % 4 == 1 and s >= 5:
                            weigh_pair(experts, (s - 5) // 4)
                    if attend is not None and s in SCORE_AT:
                        centre(attend, SCORE_AT.index(s))
                    if qkv is not None:
                        if s == 7:
                            copy_xn1(qkv)
                        if s == 10 and attend is None:
                            make_masks()
                        if s == 12:
                            copy_v(qkv)
                    if attend is not None:
                        if s == PV_AT + TILES:
                            divide(attend)
                        if s == 18:
                            add_attention(attend)
                        if s == 21:
                            normalise2(attend)
                        if s == 24:
                            pick_top(attend)
                        if s == 28:
                            weigh_top(attend)
                    if embed is not None:
                        if s == 19:
                            make_tokens(embed)
                        if s == 23:
                            normalise1(embed)
                    if attend is not None and experts is None and s == SCORE_AT[-1] + 1:
                        for n in range(2):
                            dve.wait_ge(hi_split, n + 1)
                            nc.vector.tensor_tensor(w_lo[:, n], w12[:, n], w_hi[:, n].bitcast(F32),
                                                    ALU.subtract).then_inc(lo_split, 1)

            def last(chunk):
                weigh_pair(chunk, PAIRS - 1)
                make_result(chunk)

            run_pipeline(dve, step, last)


_INS = ['x', 'L0_tok_W', 'L0_tok_b', 'L0_tok_pos_embed', 'L0_attn_w_qkv', 'L0_attn_b_qkv', 'L0_attn_w_proj',
        'L0_attn_b_proj', 'L0_ffn_gate_w', 'L0_ffn_gate_b', 'L0_ffn_w1', 'L0_ffn_w2', 'L0_ffn_w3']
_OUTS = [((4, 1024, 64), 'float32')]


def kernel(**inputs):
    import numpy as _np
    import concourse.bacc as _bacc
    from concourse import mybir as _mybir
    from concourse.bass_utils import run_bass_kernel_spmd as _run

    nc = _bacc.Bacc("TRN2", target_bir_lowering=False, num_devices=1)
    arrays, args = {}, []
    for name in _INS:
        a = _np.ascontiguousarray(inputs[name])
        arrays[f"in_{name}_dram"] = a
        args.append(nc.dram_tensor(f"in_{name}_dram", a.shape, _mybir.dt.from_np(a.dtype), kind="ExternalInput").ap())
    for i, (shape, dtype) in enumerate(_OUTS):
        dt = _mybir.dt.from_np(_np.dtype(dtype))
        args.append(nc.dram_tensor(f"out_{i}_dram", shape, dt, kind="ExternalOutput").ap())
    vit_tower(nc, *args)
    r = _run(nc, [arrays], core_ids=[0])
    return r.results[0]["out_0_dram"]
```

```python
import math
from contextlib import ExitStack

import concourse.bass as bass
from concourse import mybir

ALU = mybir.AluOpType
ACT = mybir.ActivationFunctionType
AX_X = mybir.AxisListType.X
F32 = mybir.dt.float32
F32R = mybir.dt.float32r
BF16 = mybir.dt.bfloat16
I32 = mybir.dt.int32
U32 = mybir.dt.uint32

SLOTS = 64
EACH, PAIR = 4, 8
PE_AT = {'score': (0, 2, 4, 8), 'turn_probs': (18, 20, 22, 24), 'apply_probs': (22, 24, 26, 28), 'turn_attn': 32, 'project': 34, 'turn_x2': 44, 'logits': 49, 'turn_disp': 3, 'fold': 6, 'turn_xn1': 14, 'qk': 16, 'v': (25, 28), 'frames': 31, 'patches': 34, 'embed': 39}
ACT_AT = {'exp': 11, 'probs': (19, 20, 22, 27), 'attn': 32, 'x2': 47, 'disp': 2, 'qk': 18, 'frames': 32, 'patches': 34}
DVE_AT = {'centre': (0, 1, 4, 8), 'divide': 30, 'add_attention': 35, 'normalise2': 39, 'pick_top': 50, 'weigh_top': 63, 'result': 7, 'xn1': 15, 'v': (25, 28), 'tokens': 46, 'normalise1': 53, 'stats2': 35, 'split_x2': 40, 'place_top': 52, 'stats1': 46}
POOL_AT = {'rsqrt2': 35, 'rsqrt1': 40, 'exp_top': 57, 'route': 63}
SPREAD = 5
DOWN = 9
EX_AT = {'h1': 0, 'h2': 0, 'silu': 3, 'gate': 0, 'hold': 6, 'weigh': 9, 'add': 10}
WARM = [{'patches': 2, 'embed': 2}, {'turn_xn1': 10, 'qk': 2, 'v': 2, 'patches': 4, 'embed': 2, 'frames': 0}, {'score': 1, 'turn_xn1': 7, 'qk': 2, 'v': 0, 'frames': 0, 'patches': 0, 'embed': 2, 'turn_probs': 3, 'apply_probs': 0, 'turn_attn': 0, 'project': 4, 'turn_x2': 5, 'logits': 4, 'up': 12}]
EPS = 1e-5
MASKED = -1e30


def vit_tower(nc, x, tok_W, tok_b, pos_embed, w_qkv, b_qkv, w_proj, b_proj, gate_w, gate_b, w1, w2, w3, out):
    IMAGES, _, MELS, FRAMES = x.shape
    E = tok_W.shape[0]
    PATCH = 8
    ROWS, COLS = MELS // PATCH, FRAMES // PATCH // 2
    CHUNKS = 2 * IMAGES
    T = ROWS * COLS
    TILES = T // 128
    H, DH, K = 8, E // 8, 31
    G = T // 32
    SPAN = 32 + K - 1
    PAD = K // 2
    KEYS = T + 32
    SCALE = float(DH) ** -0.5
    X, HID = gate_w.shape[1], w1.shape[2]
    PAIRS = X // 2
    PARTS = 3 * X

    with ExitStack() as ctx:
        def sb(name, shape, dt=F32):
            return ctx.enter_context(nc.sbuf_tensor(name, shape, dt))

        def bank(name):
            return ctx.enter_context(nc.psum_tensor(name, [128, 512], F32))

        def sem(name):
            return ctx.enter_context(nc.semaphore(name))

        ident = sb("ident", [128, 128])
        ident_bf = sb("ident_bf", [128, 128], BF16)
        fold = sb("fold", [128, E])
        band = sb("band", [128, KEYS])
        spread = sb("spread", [128, PAIRS, 2, 64], BF16)
        iota_x = sb("iota_x", [128, X])
        tokW = sb("tokW", [E, 64])
        tokWT = sb("tokWT", [65, E])
        pos = sb("pos", [128, TILES, 2, E])
        Wqkv = sb("Wqkv", [65, 3 * E])
        Wproj = sb("Wproj", [65, E])
        gate = sb("gate", [128, X])
        gate_bias = sb("gate_bias", [128, X])
        w12 = sb("w12", [128, 2, X, HID])
        w_hi = sb("w_hi", [128, 2, X, HID], F32R)
        w_lo = sb("w_lo", [128, 2, X, HID], F32R)
        w3s = sb("w3s", [HID, X, E])

        x_stage = sb("x_stage", [128, FRAMES])
        by_frame = sb("by_frame", [COLS, 128, PATCH])
        patchT = sb("patchT", [65, T])
        tokens = sb("tokens", [128, 2, TILES, E])
        xn1 = sb("xn1", [128, TILES, E])
        xn1T = sb("xn1T", [65, KEYS])
        qT = sb("qT", [128, T])
        kT = sb("kT", [128, T])
        k_diag = sb("k_diag", [128, H, KEYS])
        v_span = sb("v_span", [128, 2, G, H // 2, 2 * (DH + 1)])
        smax = sb("smax", [128, TILES, H])
        probs = sb("probs", [128, TILES, H, 64])
        probsT = sb("probsT", [128, 2, H // 2, 128])
        inv_sum = sb("inv_sum", [128, TILES, H])
        attn = sb("attn", [128, TILES, E])
        attnT = sb("attnT", [65, T])
        resid = sb("resid", [128, 2, TILES, E])
        xn2 = sb("xn2", [128, TILES, E])
        xn2_parts = sb("xn2_parts", [128, TILES, 2 * E], F32R)
        x2T = sb("x2T", [128, 2, T], F32R)
        logits = sb("logits", [128, TILES, X])
        top = sb("top", [128, TILES, 8])
        top_at = sb("top_at", [128, TILES, 8], U32)
        top_idx = sb("top_idx", [128, TILES, 2])
        top_diff = sb("top_diff", [128, TILES, 2])
        top_exp = sb("top_exp", [128, TILES, 2])
        e_base = sb("e_base", [128, TILES, 2])
        top_sum = sb("top_sum", [128, TILES])
        top_inv = sb("top_inv", [128, TILES])
        top_w = sb("top_w", [128, TILES, 2])
        hot = sb("hot", [128, 2, TILES, X])
        hot_w = sb("hot_w", [128, 2, TILES, X])
        disp = sb("disp", [128, 2, TILES, X])
        disp_parts = sb("disp_parts", [128, TILES, PARTS], BF16)
        dispT = sb("dispT", [128, T], BF16)
        ln = [{"stats": sb(f"stats{n}", [128, TILES, 6]), "mv": sb(f"mv{n}", [128, TILES, 2]),
               "var": sb(f"var{n}", [128, TILES]), "rstd": sb(f"rstd{n}", [128, TILES])} for n in (1, 2)]
        neg_half = sb("neg_half", [128, TILES])
        silu = sb("silu", [128, 2, T])
        hidden = sb("hidden", [128, 4, T])
        weight = sb("weight", [128, 2, T])
        y_w = sb("y_w", [128, 2, T])
        y_sum = sb("y_sum", [128, T])
        result = sb("result", [128, 2, TILES, E])

        b_h1, b_h2, b_y = [bank("b_h1a"), bank("b_h1b")], bank("b_h2"), bank("b_y")
        b_s, b_m = bank("b_s"), bank("b_m")
        b_p = [bank("b_p0"), bank("b_p1")]

        c_zero, c_tri, c_mask, c_band = sem("c_zero"), sem("c_tri"), sem("c_mask"), sem("c_band")
        c_ident, c_masks, c_rows = sem("c_ident"), sem("c_masks"), sem("c_rows")
        pe_apart, dve_apart, pool_apart = sem("pe_apart"), sem("dve_apart"), sem("pool_apart")
        d_tok, d_attn, d_ffn = sem("d_tok"), sem("d_attn"), sem("d_ffn")
        w_turned, w_copied = sem("w_turned"), sem("w_copied")
        hi_split, lo_split = sem("hi_split"), sem("lo_split")
        x_loaded, x_turned = sem("x_loaded"), sem("x_turned")
        frames_copied, patch_turned, patch_copied = sem("frames_copied"), sem("patch_turned"), sem("patch_copied")
        embedded, tokens_made = sem("embedded"), sem("tokens_made")
        ln_dve = [sem("ln1_dve"), sem("ln2_dve")]
        ln_rstd = [sem("ln1_rstd"), sem("ln2_rstd")]
        xn1_made, xn1_turned, xn1_copied = sem("xn1_made"), sem("xn1_turned"), sem("xn1_copied")
        qk_made, v_made, q_copied, k_copied, v_copied = (
            sem("qk_made"), sem("v_made"), sem("q_copied"), sem("k_copied"), sem("v_copied"))
        k_spread = sem("k_spread")
        scored, maxed, centred = sem("scored"), sem("maxed"), sem("centred")
        exped = sem("exped")
        p_turned, p_copied, pv_done = sem("p_turned"), sem("p_copied"), sem("pv_done")
        inverted, attn_made, attn_turned, attn_copied = (
            sem("inverted"), sem("attn_made"), sem("attn_turned"), sem("attn_copied"))
        projected, resid_made = sem("projected"), sem("resid_made")
        xn2_made, hi_made, lo_made = sem("xn2_made"), sem("hi_made"), sem("lo_made")
        x2_turned, x2_copied = sem("x2_turned"), sem("x2_copied")
        gated, biased, topped, top_found, idx_made, diffed, top_exped = (
            sem("gated"), sem("biased"), sem("topped"), sem("top_found"), sem("idx_made"), sem("diffed"),
            sem("top_exped"))
        idx_cast = sem("idx_cast")
        summed2, inverted2, weighed = sem("summed2"), sem("inverted2"), sem("weighed")
        routed = sem("routed")
        disp_turned, disp_copied = sem("disp_turned"), sem("disp_copied")
        h1_done, h2_done, silu_done, hid_done = sem("h1_done"), sem("h2_done"), sem("silu_done"), sem("hid_done")
        y_done, w_done, w_held, yw_done = sem("y_done"), sem("w_done"), sem("w_held"), sem("yw_done")
        summed = sem("summed")
        folded, result_made = sem("folded"), sem("result_made")
        stored = [sem("stored0"), sem("stored1")]
        ROUTE, LNS = 7, 3

        def cid(chunk):
            return 2 * chunk[0] + chunk[1]

        def wait(eng, s, n):
            if not isinstance(n, int) or n > 0:
                eng.wait_ge(s, n)

        def ahead(c, n):
            return min(c + 1 + n, CHUNKS) if isinstance(c, int) else c + 1 + n

        apart = {nc.tensor.engine: pe_apart, nc.vector.engine: dve_apart, nc.gpsimd.engine: pool_apart}

        def wait_apart(eng, s, n):
            wait(eng, s, n)
            if not isinstance(n, int):
                eng.sem_inc(apart[eng.engine], 1)

        def run_pipeline(eng, step, last):
            end = IMAGES - 1
            step(embed=(0, 0))
            step(embed=(0, 1), qkv=(0, 0))
            step(embed=(1, 0), qkv=(0, 1), attend=(0, 0))
            step(embed=(1, 1), qkv=(1, 0), attend=(0, 1), experts=(0, 0))
            with eng.Fori(1, end) as b:
                step(embed=(b + 1, 0), qkv=(b, 1), attend=(b, 0), experts=(b - 1, 1), finish=(b - 1, 0))
                step(embed=(b + 1, 1), qkv=(b + 1, 0), attend=(b, 1), experts=(b, 0), finish=(b - 1, 1))
            step(qkv=(end, 1), attend=(end, 0), experts=(end - 1, 1), finish=(end - 1, 0))
            step(attend=(end, 1), experts=(end, 0), finish=(end - 1, 1))
            step(experts=(end, 1), finish=(end, 0))
            last((end, 1))

        block = ctx.enter_context(nc.Block())

        @block.sync
        def _(sp):
            sp.dma_start(x_stage[:], x[0, 0]).then_inc(x_loaded, 16)
            sp.dma_start(pos[:], pos_embed[0].rearrange("(t p g) e -> p t g e", t=TILES, g=2)).then_inc(d_tok, 16)
            sp.dma_start(Wqkv[0:E, :], w_qkv).then_inc(d_attn, 16)
            sp.dma_start(Wqkv[64:65, :], b_qkv.rearrange("(a e) -> a e", a=1)).then_inc(d_attn, 16)
            sp.dma_start(Wproj[0:E, :], w_proj).then_inc(d_attn, 16)
            sp.dma_start(Wproj[64:65, :], b_proj.rearrange("(a e) -> a e", a=1)).then_inc(d_attn, 16)
            for half in range(2):
                sp.dma_start(gate[64 * half:64 * half + 64, :], gate_w).then_inc(d_attn, 16)
            sp.dma_start(gate_bias[:], gate_b.partition_broadcast(128)).then_inc(d_attn, 16)
            for n in range(2):
                for half in range(2):
                    sp.dma_start(w12[64 * half:64 * half + 64, n],
                                 (w1, w2)[n].rearrange("e d h -> d e h")).then_inc(d_ffn, 16)
            sp.dma_start(w3s[:], w3.rearrange("e h o -> h e o")).then_inc(d_ffn, 16)

            def load_image(b):
                sp.wait_ge(x_turned, 2 * b)
                sp.dma_start(x_stage[:], x[b, 0]).then_inc(x_loaded, 16)

            def spread_keys(chunk):
                sp.wait_ge(k_copied, cid(chunk) + 1)
                for h in range(H):
                    sp.dma_start(k_diag[DH * h:DH * h + DH, h, PAD:PAD + T],
                                 kT[64 + DH * h:64 + DH * h + DH, :]).then_inc(k_spread, 16)

            def store(chunk):
                b, g = chunk
                sp.wait_ge(result_made, cid(chunk) + 1)
                sp.dma_start(out[b].rearrange("(t p g) e -> g p t e", t=TILES, g=2)[g],
                             result[:, g]).then_inc(stored[g], 16)

            sp.wait_ge(c_rows, 3)
            spread_keys((0, 0))
            load_image(1)
            spread_keys((0, 1))
            spread_keys((1, 0))
            with sp.Fori(1, IMAGES - 1) as b:
                store((b - 1, 0))
                load_image(b + 1)
                spread_keys((b, 1))
                store((b - 1, 1))
                spread_keys((b + 1, 0))
            store((IMAGES - 2, 0))
            spread_keys((IMAGES - 1, 1))
            store((IMAGES - 2, 1))
            store((IMAGES - 1, 0))
            store((IMAGES - 1, 1))
            for g in range(2):
                sp.wait_ge(stored[g], 16 * IMAGES)

        @block.gpsimd
        def _(pool):
            pool.memset(ident[:], 0.0).then_inc(c_zero, 1)
            pool.wait_ge(c_zero, 1)
            pool.affine_select(out=ident[:], in_=ident[:], compare_op=ALU.not_equal, fill=1.0, base=0,
                               pattern=[[-1, 128]], channel_multiplier=1).then_inc(c_ident, 1)
            pool.memset(neg_half[:], -0.5)
            pool.memset(e_base[:], math.e).then_inc(c_zero, 1)
            pool.wait_ge(c_ident, 1)
            pool.tensor_copy(ident_bf[:], ident[:]).then_inc(c_tri, 1)

            steps = [0]

            def keep(odd, blocks, base, mult, step, fill):
                pool.wait_ge(c_mask, steps[0])
                n = blocks.stop - blocks.start
                part = band[64 + 32 * odd:96 + 32 * odd, 32 * odd + 64 * blocks.start:32 * odd + 64 * blocks.stop]
                pool.affine_select(out=part, in_=part, compare_op=ALU.is_ge, fill=fill, base=base,
                                   pattern=[[0, n], [step, 64]], channel_multiplier=mult).then_inc(c_mask, 1)
                steps[0] += 1

            pool.memset(band[:], 0.0).then_inc(c_mask, 1)
            steps[0] += 1
            for odd, blocks in ((0, slice(1, G // 2)), (1, slice(0, G // 2 - 1))):
                keep(odd, blocks, 0, -1, 1, MASKED)
                keep(odd, blocks, K - 1, 1, -1, MASKED)
            keep(0, slice(0, 1), PAD + K - 1, 0, -1, MASKED)
            keep(0, slice(0, 1), -K, -1, 1, 0.0)
            keep(0, slice(0, 1), 0, -1, 1, MASKED)
            keep(0, slice(0, 1), -PAD, 0, 1, MASKED)
            last = slice(G // 2 - 1, G // 2)
            keep(1, last, -(PAD + 1), 0, 1, MASKED)
            keep(1, last, -1, 1, -1, 0.0)
            keep(1, last, K - 1, 1, -1, MASKED)
            keep(1, last, PAD + K, 0, -1, MASKED)
            pool.wait_ge(c_tri, 1)
            pool.wait_ge(c_mask, steps[0])
            pool.memset(fold[:], 0.0).then_inc(c_band, 1)

            def make_fold_and_spread():
                pool.memset(spread[:], 0.0).then_inc(c_zero, 1)
                pool.wait_ge(c_band, 1)
                for k in range(2):
                    pool.affine_select(out=fold[:], in_=fold[:], compare_op=ALU.not_equal, fill=1.0, base=-E * k,
                                       pattern=[[-1, E]], channel_multiplier=1).then_inc(c_tri, 1)
                    pool.wait_ge(c_tri, k + 2)
                pool.wait_ge(c_zero, 3)
                for part in range(3):
                    pool.affine_select(out=spread[:], in_=spread[:], compare_op=ALU.not_equal, fill=1.0,
                                       base=-X * part, pattern=[[-2, PAIRS], [-1, 2], [0, 64]],
                                       channel_multiplier=1).then_inc(c_mask, 1)
                    steps[0] += 1
                    pool.wait_ge(c_mask, steps[0])
                pool.iota(iota_x[:], pattern=[[1, X]], base=0, channel_multiplier=0,
                          allow_small_or_imprecise_dtypes=True).then_inc(c_band, 1)

            def split_low():
                for n in range(2):
                    pool.wait_ge(hi_split, n + 1)
                    pool.tensor_tensor(w_lo[:, n], w12[:, n], w_hi[:, n].bitcast(F32),
                                       ALU.subtract).then_inc(lo_split, 1)

            def rsqrt(n, c):
                pool.wait_ge(ln_dve[n], LNS * c + 3)
                pool.tensor_tensor(ln[n]["rstd"][:], ln[n]["var"][:], neg_half[:], ALU.pow).then_inc(ln_rstd[n], 1)

            def exp_top(c):
                pool.wait_ge(diffed, c + 1)
                pool.tensor_tensor(top_exp[:], e_base[:], top_diff[:], ALU.pow).then_inc(top_exped, 1)

            def route(c):
                pool.wait_ge(idx_made, c + 1)
                pool.wait_ge(weighed, c + 1)
                for k in range(2):
                    pool.tensor_tensor(hot_w[:, k], hot[:, k],
                                       top_w[:, :, k].unsqueeze(2).to_broadcast([128, TILES, X]),
                                       ALU.mult).then_inc(routed, 1)
                pool.wait_ge(routed, ROUTE * c + 2)
                pool.tensor_tensor(disp[:, 0], hot_w[:, 0], hot_w[:, 1], ALU.add).then_inc(routed, 1)
                wait(pool, disp_turned, c)
                for k in range(2):
                    part = disp_parts[:, :, X * k:X * k + X]
                    wait_apart(pool, routed, ROUTE * c + 3 + 2 * k)
                    pool.tensor_copy(part, disp[:, k]).then_inc(routed, 1)
                    pool.wait_ge(routed, ROUTE * c + 4 + 2 * k)
                    rest = disp[:, 1] if k == 0 else disp_parts[:, :, 2 * X:3 * X]
                    pool.tensor_tensor(rest, disp[:, k], part, ALU.subtract).then_inc(routed, 1)

            def add_pair(c, q):
                pool.wait_ge(yw_done, PAIRS * c + q + 1)
                if q == 1:
                    wait(pool, folded, c)
                    pool.tensor_tensor(y_sum[:], y_w[:, 0], y_w[:, 1], ALU.add).then_inc(summed, 1)
                else:
                    pool.wait_ge(summed, (PAIRS - 1) * c + q - 1)
                    pool.tensor_tensor(y_sum[:], y_sum[:], y_w[:, q % 2], ALU.add).then_inc(summed, 1)

            def step(embed=None, qkv=None, attend=None, experts=None, finish=None):
                if attend is not None and experts is None:
                    make_fold_and_spread()
                    split_low()
                for s in range(SLOTS):
                    if attend is not None:
                        if s == POOL_AT["rsqrt2"]:
                            rsqrt(1, cid(attend))
                        if s == POOL_AT["exp_top"]:
                            exp_top(cid(attend))
                    if embed is not None and s == POOL_AT["rsqrt1"]:
                        rsqrt(0, cid(embed))
                    if finish is not None and s == EX_AT["add"] - PAIR:
                        add_pair(cid(finish), PAIRS - 1)
                    if experts is not None and s % PAIR == EX_AT["add"] % PAIR and s > EX_AT["add"]:
                        add_pair(cid(experts), (s - EX_AT["add"]) // PAIR)
                    if attend is not None and s == POOL_AT["route"]:
                        route(cid(attend))

            run_pipeline(pool, step, lambda chunk: add_pair(cid(chunk), PAIRS - 1))

        @block.tensor
        def _(pe):
            pe.wait_ge(c_ident, 1)
            pe.wait_ge(d_tok, 48)
            pe.transpose(b_s[0:64, 0:E], tokW[:], ident[0:E, 0:E]).then_inc(w_turned, 1)
            pe.wait_ge(c_tri, 1)

            def turn_frames(chunk):
                b, g = chunk
                c = cid(chunk)
                pe.wait_ge(x_loaded, 16 * b + 16)
                if isinstance(c, int) and c == 1:
                    pe.wait_ge(tokens_made, c)
                wait(pe, p_copied, TILES * (c - 1))
                cols = x_stage[:].rearrange("r (f g j) -> r g j f", g=2, j=PATCH)[:, g]
                for j in range(PATCH):
                    ins = pe.transpose(b_p[j // 4][0:COLS, 128 * (j % 4):128 * (j % 4) + 128], cols[:, j],
                                       ident[:])
                ins.then_inc(x_turned, 1)

            def turn_patches(chunk):
                c = cid(chunk)
                wait_apart(pe, frames_copied, c + 1)
                for m in range(ROWS):
                    ins = pe.transpose(b_p[0][0:64, COLS * m:COLS * m + COLS],
                                       by_frame[:, PATCH * m:PATCH * m + PATCH].rearrange("f i j -> f (i j)"),
                                       ident[0:COLS, 0:COLS])
                ins.then_inc(patch_turned, 1)

            def embed_patches(chunk):
                c = cid(chunk)
                if isinstance(c, int) and c == 0:
                    pe.wait_ge(w_copied, 1)
                    pe.wait_ge(c_rows, 1)
                pe.wait_ge(patch_copied, c + 1)
                for t in range(TILES):
                    ins = pe.matmul(b_p[1][:, E * t:E * t + E], patchT[:, 128 * t:128 * t + 128], tokWT[:],
                                    start=True, stop=True)
                ins.then_inc(embedded, 1)

            def turn_xn1(chunk):
                wait(pe, centred, TILES * cid(chunk))
                wait_apart(pe, xn1_made, cid(chunk) + 1)
                for t in range(TILES):
                    ins = pe.transpose(b_s[0:E, 128 * t:128 * t + 128], xn1[:, t], ident[:])
                ins.then_inc(xn1_turned, 1)

            def make_qk(chunk):
                c = cid(chunk)
                if isinstance(c, int) and c == 0:
                    pe.wait_ge(d_attn, 16 * 7)
                pe.wait_ge(xn1_copied, c + 1)
                pe.matmul(b_s[:], Wqkv[:, 0:2 * E], xn1T[:, PAD:PAD + T], start=True, stop=True).then_inc(qk_made, 1)

            def make_v(chunk, half):
                c = cid(chunk)
                if half == 0:
                    pe.wait_ge(q_copied, c + 1)
                    pe.wait_ge(k_copied, c + 1)
                else:
                    pe.wait_ge(v_copied, 2 * c + 1)
                for j in range(G // 2):
                    k0 = 32 * (G // 2 * half + j)
                    ins = pe.matmul(b_s[0:SPAN, E * j:E * j + E], xn1T[:, k0:k0 + SPAN], Wqkv[:, 2 * E:3 * E],
                                    start=True, stop=True)
                ins.then_inc(v_made, 1)

            def score(chunk, t):
                c = cid(chunk)
                dst = (b_s, b_p[0], b_p[1], b_s)[t][:, 0:H * SPAN]
                if t == 0:
                    if isinstance(c, int) and c == 0:
                        pe.wait_ge(c_masks, 1)
                        pe.wait_ge(c_rows, 3)
                    pe.wait_ge(k_spread, 16 * H * (c + 1))
                    pe.wait_ge(q_copied, c + 1)
                    pe.wait_ge(v_copied, 2 * c + 2)
                    wait(pe, x2_copied, c)
                if t == 1:
                    pe.wait_ge(patch_copied, ahead(c, 1))
                if t == 2:
                    pe.wait_ge(tokens_made, ahead(c, 1))
                if t == 3:
                    pe.wait_ge(centred, TILES * c + 1)
                for g in range(4):
                    q0 = 128 * t + 32 * g
                    ins = pe.matmul(dst[32 * g:32 * g + 32, :], qT[:, q0:q0 + 32], k_diag[:, :, q0:q0 + SPAN],
                                    start=True, stop=True)
                ins.then_inc(scored, 1)

            def turn_probs(chunk, t):
                c = cid(chunk)
                if t == 0:
                    wait_apart(pe, exped, c + 1)
                if t >= 2:
                    wait_apart(pe, p_copied, TILES * c + t - 1)
                for k in range(H // 2):
                    ins = pe.transpose(b_p[t % 2][:, 128 * k:128 * k + 128],
                                       probs[:, t, 2 * k:2 * k + 2].rearrange("p h k -> p (h k)"), ident[:])
                ins.then_inc(p_turned, 1)

            def apply_probs(chunk, t):
                c = cid(chunk)
                pe.wait_ge(p_copied, TILES * c + t + 1)
                if t == 0:
                    wait(pe, disp_copied, c)
                    wait(pe, result_made, c - 1)
                o = b_m[:, 0:TILES * H * (DH + 1)].rearrange("p (t k d) -> p t k d", t=TILES, k=H // 2)
                for k in range(H // 2):
                    for g in range(4):
                        ins = pe.matmul(o[32 * g:32 * g + 32, t, k], probsT[:, t % 2, k, 32 * g:32 * g + 32],
                                        v_span[:, chunk[1], 4 * t + g, k], start=True, stop=True)
                ins.then_inc(pv_done, 1)

            def turn_attn(chunk):
                pe.wait_ge(attn_made, cid(chunk) + 1)
                wait_apart(pe, v_copied, 2 * ahead(cid(chunk), 1))
                for t in range(TILES):
                    ins = pe.transpose(b_s[0:E, 128 * t:128 * t + 128], attn[:, t], ident[:])
                ins.then_inc(attn_turned, 1)

            def project(chunk):
                pe.wait_ge(attn_copied, cid(chunk) + 1)
                for t in range(TILES):
                    ins = pe.matmul(b_m[:, E * t:E * t + E], attnT[:, 128 * t:128 * t + 128], Wproj[:],
                                    start=True, stop=True)
                ins.then_inc(projected, 1)

            def turn_x2(chunk):
                pe.wait_ge(hi_made, cid(chunk) + 1)
                pe.wait_ge(lo_made, cid(chunk) + 1)
                for t in range(TILES):
                    ins = pe.transpose(b_s[:, 128 * t:128 * t + 128], xn2_parts[:, t].bitcast(F32), ident[:])
                ins.then_inc(x2_turned, 1)

            def make_logits(chunk):
                b, g = chunk
                pe.wait_ge(x2_copied, cid(chunk) + 1)
                for t in range(TILES):
                    ins = pe.matmul(b_m[:, X * t:X * t + X], x2T[:, g, 128 * t:128 * t + 128].bitcast(F32),
                                    gate[:], start=True, stop=True)
                ins.then_inc(gated, 1)

            def turn_disp(chunk):
                wait_apart(pe, routed, ROUTE * (cid(chunk) + 1))
                dst = b_m[:].bitcast(BF16)
                for t in range(TILES):
                    ins = pe.transpose(dst[0:PARTS, 128 * t:128 * t + 128], disp_parts[:, t], ident_bf[:])
                ins.then_inc(disp_turned, 1)

            def up(chunk, e, n):
                b, g = chunk
                c = cid(chunk)
                if e == 0 and n == 0:
                    pe.wait_ge(x2_copied, c + 1)
                    if isinstance(c, int) and c == 0:
                        pe.wait_ge(hi_split, 2)
                        pe.wait_ge(lo_split, 2)
                if n == 0:
                    dst, made = b_h1[e % 2], h1_done
                    wait(pe, silu_done, X * c + e - 1)
                else:
                    dst, made = b_h2, h2_done
                    wait(pe, hid_done, X * c + e)
                pe.matmul(dst[:], w_hi[:, n, e], x2T[:, g], start=True, stop=False)
                pe.matmul(dst[:], w_lo[:, n, e], x2T[:, g], start=False, stop=True).then_inc(made, 1)

            def down(chunk, q):
                c = cid(chunk)
                pe.wait_ge(hid_done, X * c + 2 * q + 2)
                pe.wait_ge(w_held, PAIRS * c + q + 1)
                for k in range(2):
                    ins = pe.matmul(b_y[64 * k:64 * k + 64, :], w3s[:, 2 * q + k], hidden[:, (2 * q + k) % 4],
                                    start=True, stop=True)
                ins.then_inc(y_done, 1)

            def spread_weights(chunk, q):
                c = cid(chunk)
                if q == 0:
                    pe.wait_ge(disp_copied, c + 1)
                    if isinstance(c, int) and c == 0:
                        pe.wait_ge(c_band, 2)
                wait(pe, yw_done, PAIRS * c + q)
                pe.matmul(b_y[:], spread[:, q].rearrange("p a b -> p (a b)"), dispT[:], start=True,
                          stop=True).then_inc(w_done, 1)

            def fold_pairs(chunk):
                c = cid(chunk)
                pe.wait_ge(summed, (PAIRS - 1) * (c + 1))
                pe.wait_ge(disp_copied, ahead(c, 1))
                for t in range(TILES):
                    ins = pe.matmul(b_m[:, E * t:E * t + E], y_sum[:, 128 * t:128 * t + 128], fold[:],
                                    start=True, stop=True)
                ins.then_inc(folded, 1)

            def step(embed=None, qkv=None, attend=None, experts=None, finish=None):
                fill = {} if experts is not None or attend is None and embed is None else WARM[
                    (qkv is not None) + (attend is not None)]

                def warm(stage):
                    for _ in range(fill.get(stage, 0)):
                        pe.matmul(b_h2[:], ident_bf[:], ident_bf[:].unsqueeze(1).to_broadcast([128, 4, 128]),
                                  start=True, stop=True)

                for s in range(SLOTS):
                    if experts is not None:
                        if s % EACH == EX_AT["h1"] and s // EACH + 1 < X:
                            up(experts, s // EACH + 1, 0)
                        if s % EACH == EX_AT["h2"]:
                            up(experts, s // EACH, 1)
                        if s % PAIR == SPREAD:
                            spread_weights(experts, s // PAIR)
                        if s % PAIR == DOWN % PAIR and s >= DOWN:
                            down(experts, (s - DOWN) // PAIR)
                        if s == PE_AT["turn_disp"]:
                            turn_disp(experts)
                    if finish is not None:
                        if s == DOWN - PAIR:
                            down(finish, PAIRS - 1)
                        if s == PE_AT["fold"]:
                            fold_pairs(finish)
                    if attend is not None:
                        if s in PE_AT["score"]:
                            if s == PE_AT["score"][0]:
                                warm("score")
                            score(attend, PE_AT["score"].index(s))
                        if s in PE_AT["apply_probs"]:
                            if s == PE_AT["apply_probs"][0]:
                                warm("apply_probs")
                            apply_probs(attend, PE_AT["apply_probs"].index(s))
                        if s in PE_AT["turn_probs"]:
                            if s == PE_AT["turn_probs"][0]:
                                warm("turn_probs")
                            turn_probs(attend, PE_AT["turn_probs"].index(s))
                        if s == PE_AT["turn_attn"]:
                            warm("turn_attn")
                            turn_attn(attend)
                        if s == PE_AT["project"]:
                            warm("project")
                            project(attend)
                        if s == PE_AT["turn_x2"]:
                            warm("turn_x2")
                            turn_x2(attend)
                        if s == PE_AT["logits"]:
                            warm("logits")
                            make_logits(attend)
                        if s == SLOTS - 2:
                            warm("up")
                            up(attend, 0, 0)
                    if qkv is not None:
                        if s == PE_AT["turn_xn1"]:
                            warm("turn_xn1")
                            turn_xn1(qkv)
                        if s == PE_AT["qk"]:
                            warm("qk")
                            make_qk(qkv)
                        if s in PE_AT["v"]:
                            warm("v")
                            make_v(qkv, PE_AT["v"].index(s))
                    if embed is not None:
                        if s == PE_AT["frames"]:
                            warm("frames")
                            turn_frames(embed)
                        if s == PE_AT["patches"]:
                            warm("patches")
                            turn_patches(embed)
                        if s == PE_AT["embed"]:
                            warm("embed")
                            embed_patches(embed)

            def last(chunk):
                down(chunk, PAIRS - 1)
                fold_pairs(chunk)

            run_pipeline(pe, step, last)

        @block.scalar
        def _(act):
            act.dma_start(tokW[:], tok_W).then_inc(d_tok, 16)
            act.dma_start(tokWT[64:65, :], tok_b.rearrange("(a e) -> a e", a=1)).then_inc(d_tok, 16)
            act.wait_ge(w_turned, 1)
            nc.scalar.copy(tokWT[0:64, :], b_s[0:64, 0:E]).then_inc(w_copied, 1)

            def copy_frames(chunk):
                c = cid(chunk)
                act.wait_ge(x_turned, c + 1)
                wait(act, patch_turned, c)
                for k in range(2):
                    ins = nc.scalar.copy(by_frame[:, :, 4 * k:4 * k + 4].rearrange("f r j -> f j r"),
                                         b_p[k][0:COLS, :].rearrange("f (j r) -> f j r", j=4))
                ins.then_inc(frames_copied, 1)

            def copy_patches(chunk):
                c = cid(chunk)
                act.wait_ge(patch_turned, c + 1)
                wait(act, embedded, c)
                nc.scalar.copy(patchT[0:64, :], b_p[0][0:64, :]).then_inc(patch_copied, 1)

            def copy_qk(chunk):
                c = cid(chunk)
                act.wait_ge(qk_made, c + 1)
                if isinstance(c, int) and c == 0:
                    act.wait_ge(c_rows, 3)
                wait(act, k_spread, 16 * H * c)
                nc.scalar.copy(kT[64:128, :], b_s[64:128, :]).then_inc(k_copied, 1)
                nc.scalar.mul(qT[0:64, :], b_s[0:64, :], SCALE).then_inc(q_copied, 1)

            def exp_scores(chunk):
                c = cid(chunk)
                act.wait_ge(centred, TILES * (c + 1))
                spans = probs[:].rearrange("p t h k -> p (t h) k")[:, :, 0:SPAN]
                nc.scalar.activation(spans, spans, ACT.Exp).then_inc(exped, 1)

            def copy_probs(chunk, t):
                n = TILES * cid(chunk) + t
                act.wait_ge(p_turned, n + 1)
                wait(act, pv_done, n - 1)
                nc.scalar.copy(probsT[:, t % 2].rearrange("p k q -> p (k q)"), b_p[t % 2][:]).then_inc(p_copied, 1)

            def copy_attn(chunk):
                act.wait_ge(attn_turned, cid(chunk) + 1)
                nc.scalar.copy(attnT[0:E, :], b_s[0:E, :]).then_inc(attn_copied, 1)

            def copy_x2(chunk):
                b, g = chunk
                act.wait_ge(x2_turned, cid(chunk) + 1)
                nc.scalar.copy(x2T[:, g], b_s[:]).then_inc(x2_copied, 1)

            def copy_disp(chunk):
                c = cid(chunk)
                act.wait_ge(disp_turned, c + 1)
                wait(act, w_done, PAIRS * c)
                nc.scalar.copy(dispT[0:PARTS, :], b_m[:].bitcast(BF16)[0:PARTS, 0:T]).then_inc(disp_copied, 1)

            def silu_up(chunk, e):
                n = X * cid(chunk) + e
                act.wait_ge(h1_done, n + 1)
                wait(act, hid_done, n - 1)
                nc.scalar.activation(silu[:, e % 2], b_h1[e % 2][:], ACT.Silu).then_inc(silu_done, 1)

            def hold_weights(chunk, q):
                n = PAIRS * cid(chunk) + q
                act.wait_ge(w_done, n + 1)
                wait(act, yw_done, n - 1)
                nc.scalar.copy(weight[:, q % 2], b_y[:]).then_inc(w_held, 1)

            def step(embed=None, qkv=None, attend=None, experts=None, finish=None):
                for s in range(SLOTS):
                    if experts is not None:
                        if s % EACH == EX_AT["silu"] and s // EACH + 1 < X:
                            silu_up(experts, s // EACH + 1)
                        if s % PAIR == EX_AT["hold"]:
                            hold_weights(experts, s // PAIR)
                        if s == ACT_AT["disp"]:
                            copy_disp(experts)
                    if attend is not None:
                        if s == ACT_AT["exp"]:
                            exp_scores(attend)
                        if s in ACT_AT["probs"]:
                            copy_probs(attend, ACT_AT["probs"].index(s))
                        if s == ACT_AT["attn"]:
                            copy_attn(attend)
                        if s == ACT_AT["x2"]:
                            copy_x2(attend)
                        if s == SLOTS - 2:
                            silu_up(attend, 0)
                    if qkv is not None and s == ACT_AT["qk"]:
                        copy_qk(qkv)
                    if embed is not None:
                        if s == ACT_AT["frames"]:
                            copy_frames(embed)
                        if s == ACT_AT["patches"]:
                            copy_patches(embed)
                if attend is None and qkv is None and embed is not None:
                    act.wait_ge(c_band, 1)
                    nc.scalar.copy(k_diag[64:128],
                                   band[64:128, :].unsqueeze(1).to_broadcast([64, H, KEYS])).then_inc(c_masks, 1)
                if attend is None and qkv is not None:
                    act.wait_ge(d_ffn, 16 * 5)
                    for n in range(2):
                        nc.scalar.copy(w_hi[:, n].rearrange("p e h -> p (e h)"),
                                       w12[:, n].rearrange("p e h -> p (e h)")).then_inc(hi_split, 1)

            run_pipeline(act, step, lambda chunk: None)

        @block.vector
        def _(dve):
            nc.vector.memset(patchT[64:65, :], 1.0)
            nc.vector.memset(xn1T[64:65, :], 1.0)
            nc.vector.memset(attnT[64:65, :], 1.0).then_inc(c_rows, 1)
            nc.vector.memset(qT[64:128, :], 0.0)
            nc.vector.memset(v_span[:], 0.0).then_inc(c_rows, 1)
            nc.vector.memset(xn1T[0:E, 0:PAD], 0.0)
            nc.vector.memset(xn1T[0:E, PAD + T:KEYS], 0.0)
            nc.vector.memset(dispT[:], 0.0)
            nc.vector.memset(probs[:, :, :, SPAN:64], 0.0)
            dve.wait_ge(c_rows, 2)
            for r in range(2):
                nc.vector.memset(v_span[64 * r:64 * r + 64, :, :, :, (DH + 1) * r + DH], 1.0)
            dve.wait_ge(c_ident, 1)
            for odd in range(2):
                rows = slice(64 + 32 * odd, 96 + 32 * odd)
                nc.vector.tensor_copy(qT[rows, :].rearrange("i (m o q) -> i m o q", o=2, q=32)[:, :, odd],
                                      ident[rows, rows].unsqueeze(1).to_broadcast([32, G // 2, 32]))
            nc.vector.memset(k_diag[0:64], 0.0).then_inc(c_rows, 1)
            dve.wait_ge(c_rows, 3)
            dve.wait_ge(d_tok, 48)

            def stats(n, src, c):
                d, s = ln[n], ln_dve[n]
                for t in range(TILES):
                    ins = nc.vector.bn_stats(d["stats"][:, t], src[:, t])
                ins.then_inc(s, 1)
                wait_apart(dve, s, LNS * c + 1)
                for t in range(TILES):
                    ins = nc.vector.bn_aggr(d["mv"][:, t], d["stats"][:, t])
                ins.then_inc(s, 1)
                dve.wait_ge(s, LNS * c + 2)
                nc.vector.tensor_scalar(d["var"][:], d["mv"][:, :, 1], EPS, None, ALU.add).then_inc(s, 1)

            def normalise(n, dst, src, c, made):
                d = ln[n]
                dve.wait_ge(ln_rstd[n], c + 1)
                for t in range(TILES):
                    ins = nc.vector.tensor_scalar(dst[:, t], src[:, t], d["mv"][:, t, 0:1],
                                                  d["rstd"][:, t:t + 1], ALU.subtract, ALU.mult)
                ins.then_inc(made, 1)

            def make_tokens(chunk):
                b, g = chunk
                c = cid(chunk)
                dve.wait_ge(embedded, c + 1)
                nc.vector.tensor_tensor(tokens[:, g], b_p[1][:, 0:TILES * E].rearrange("p (t e) -> p t e", t=TILES),
                                        pos[:, :, g], ALU.add).then_inc(tokens_made, 1)

            def stats1(chunk):
                dve.wait_ge(tokens_made, cid(chunk) + 1)
                stats(0, tokens[:, chunk[1]], cid(chunk))

            def normalise1(chunk):
                b, g = chunk
                c = cid(chunk)
                wait(dve, xn1_turned, c)
                normalise(0, xn1, tokens[:, g], c, xn1_made)

            def copy_xn1(chunk):
                c = cid(chunk)
                wait(dve, v_made, 2 * c)
                dve.wait_ge(xn1_turned, c + 1)
                nc.vector.tensor_copy(xn1T[0:E, PAD:PAD + T], b_s[0:E, :]).then_inc(xn1_copied, 1)

            def copy_v(chunk, half):
                c = cid(chunk)
                if half == 0:
                    wait(dve, pv_done, TILES * (c - 1))
                dve.wait_ge(v_made, 2 * c + half + 1)
                V = b_s[0:SPAN, :].rearrange("p (j k r d) -> p r j k d", r=2, k=H // 2, d=DH)
                for r in range(2):
                    ins = nc.vector.tensor_copy(
                        v_span[64 * r:64 * r + SPAN, chunk[1], G // 2 * half:G // 2 * (half + 1), :,
                               (DH + 1) * r:(DH + 1) * r + DH], V[:, r])
                ins.then_inc(v_copied, 1)

            def centre(chunk, t):
                n = TILES * cid(chunk) + t
                src = (b_s, b_p[0], b_p[1], b_s)[t][:, 0:H * SPAN].rearrange("p (h k) -> p h k", h=H)
                dve.wait_ge(scored, n + 1)
                nc.vector.tensor_reduce(smax[:, t], src, AX_X, ALU.max).then_inc(maxed, 1)
                if t == 0:
                    wait(dve, p_turned, n)
                dve.wait_ge(maxed, n + 1)
                nc.vector.tensor_tensor(probs[:, t, :, 0:SPAN], src,
                                        smax[:, t].unsqueeze(2).to_broadcast([128, H, SPAN]),
                                        ALU.subtract).then_inc(centred, 1)

            def divide(chunk):
                c = cid(chunk)
                dve.wait_ge(pv_done, TILES * (c + 1))
                o = b_m[:, 0:TILES * H * (DH + 1)].rearrange("p (th d) -> p th d", d=DH + 1)
                nc.vector.reciprocal(inv_sum[:].rearrange("p t h -> p (t h)"), o[:, :, DH]).then_inc(inverted, 1)
                dve.wait_ge(inverted, c + 1)
                nc.vector.tensor_tensor(
                    attn[:].rearrange("p t (h d) -> p (t h) d", d=DH), o[:, :, 0:DH],
                    inv_sum[:].rearrange("p t h -> p (t h)").unsqueeze(2).to_broadcast([128, TILES * H, DH]),
                    ALU.mult).then_inc(attn_made, 1)

            def add_attention(chunk):
                b, g = chunk
                c = cid(chunk)
                dve.wait_ge(projected, c + 1)
                nc.vector.tensor_tensor(resid[:, g], b_m[:, 0:TILES * E].rearrange("p (t e) -> p t e", t=TILES),
                                        tokens[:, g], ALU.add).then_inc(resid_made, 1)

            def stats2(chunk):
                dve.wait_ge(resid_made, cid(chunk) + 1)
                stats(1, resid[:, chunk[1]], cid(chunk))

            def normalise2(chunk):
                normalise(1, xn2, resid[:, chunk[1]], cid(chunk), xn2_made)

            def split_x2(chunk):
                c = cid(chunk)
                dve.wait_ge(xn2_made, c + 1)
                nc.vector.tensor_copy(xn2_parts[:, :, 0:E], xn2[:]).then_inc(hi_made, 1)
                dve.wait_ge(hi_made, c + 1)
                nc.vector.tensor_tensor(xn2_parts[:, :, E:2 * E], xn2[:], xn2_parts[:, :, 0:E].bitcast(F32),
                                        ALU.subtract).then_inc(lo_made, 1)

            def pick_top(chunk):
                c = cid(chunk)
                dve.wait_ge(gated, c + 1)
                if isinstance(c, int) and c == 0:
                    dve.wait_ge(d_attn, 16 * 7)
                nc.vector.tensor_tensor(
                    logits[:], b_m[:, 0:TILES * X].rearrange("p (t x) -> p t x", t=TILES),
                    gate_bias[:].unsqueeze(1).to_broadcast([128, TILES, X]), ALU.add).then_inc(biased, 1)
                wait_apart(dve, biased, c + 1)
                for t in range(TILES):
                    ins = nc.vector.max(top[:, t], logits[:, t])
                ins.then_inc(topped, 1)
                dve.wait_ge(topped, c + 1)
                nc.vector.tensor_tensor(top_diff[:], top[:, :, 0:2],
                                        top[:, :, 0:1].to_broadcast([128, TILES, 2]),
                                        ALU.subtract).then_inc(diffed, 1)

            def place_top(chunk):
                c = cid(chunk)
                for t in range(TILES):
                    ins = nc.vector.max_index(top_at[:, t], top[:, t], logits[:, t])
                ins.then_inc(top_found, 1)
                dve.wait_ge(top_found, c + 1)
                nc.vector.tensor_copy(top_idx[:], top_at[:, :, 0:2]).then_inc(idx_cast, 1)
                dve.wait_ge(idx_cast, c + 1)
                if isinstance(c, int) and c == 0:
                    dve.wait_ge(c_band, 2)
                wait(dve, routed, ROUTE * c)
                for k in range(2):
                    ins = nc.vector.tensor_tensor(
                        hot[:, k], iota_x[:].unsqueeze(1).to_broadcast([128, TILES, X]),
                        top_idx[:, :, k].unsqueeze(2).to_broadcast([128, TILES, X]), ALU.is_equal)
                ins.then_inc(idx_made, 1)

            def weigh_top(chunk):
                c = cid(chunk)
                dve.wait_ge(top_exped, c + 1)
                nc.vector.tensor_tensor(top_sum[:], top_exp[:, :, 0], top_exp[:, :, 1], ALU.add).then_inc(summed2, 1)
                dve.wait_ge(summed2, c + 1)
                nc.vector.reciprocal(top_inv[:], top_sum[:]).then_inc(inverted2, 1)
                dve.wait_ge(inverted2, c + 1)
                nc.vector.tensor_tensor(top_w[:], top_exp[:],
                                        top_inv[:].unsqueeze(2).to_broadcast([128, TILES, 2]),
                                        ALU.mult).then_inc(weighed, 1)

            def gate_hidden(chunk, e):
                n = X * cid(chunk) + e
                dve.wait_ge(silu_done, n + 1)
                dve.wait_ge(h2_done, n + 1)
                wait(dve, y_done, PAIRS * cid(chunk) + e // 2 - 1)
                nc.vector.tensor_tensor(hidden[:, e % 4], silu[:, e % 2], b_h2[:], ALU.mult).then_inc(hid_done, 1)

            def weigh_pair(chunk, q):
                c = cid(chunk)
                n = PAIRS * c + q
                dve.wait_ge(y_done, n + 1)
                dve.wait_ge(w_held, n + 1)
                wait(dve, summed, (PAIRS - 1) * c + (q - 1 if q < 2 else max(q - 2, 1)))
                nc.vector.tensor_tensor(y_w[:, q % 2], b_y[:], weight[:, q % 2], ALU.mult).then_inc(yw_done, 1)

            def make_result(chunk):
                b, g = chunk
                c = cid(chunk)
                dve.wait_ge(folded, c + 1)
                wait(dve, stored[g], 16 * b)
                nc.vector.tensor_tensor(result[:, g], b_m[:, 0:TILES * E].rearrange("p (t e) -> p t e", t=TILES),
                                        resid[:, g], ALU.add).then_inc(result_made, 1)

            def step(embed=None, qkv=None, attend=None, experts=None, finish=None):
                for s in range(SLOTS):
                    if finish is not None:
                        if s == EX_AT["weigh"] - PAIR:
                            weigh_pair(finish, PAIRS - 1)
                        if s == DVE_AT["result"]:
                            make_result(finish)
                    if experts is not None:
                        if s % EACH == EX_AT["gate"]:
                            gate_hidden(experts, s // EACH)
                        if s % PAIR == EX_AT["weigh"] % PAIR and s >= EX_AT["weigh"]:
                            weigh_pair(experts, (s - EX_AT["weigh"]) // PAIR)
                    if attend is not None and s in DVE_AT["centre"]:
                        centre(attend, DVE_AT["centre"].index(s))
                    if qkv is not None:
                        if s == DVE_AT["xn1"]:
                            copy_xn1(qkv)
                        if s in DVE_AT["v"]:
                            copy_v(qkv, DVE_AT["v"].index(s))
                    if attend is not None:
                        if s == DVE_AT["divide"]:
                            divide(attend)
                        if s == DVE_AT["add_attention"]:
                            add_attention(attend)
                        if s == DVE_AT["stats2"]:
                            stats2(attend)
                        if s == DVE_AT["normalise2"]:
                            normalise2(attend)
                        if s == DVE_AT["split_x2"]:
                            split_x2(attend)
                        if s == DVE_AT["pick_top"]:
                            pick_top(attend)
                        if s == DVE_AT["place_top"]:
                            place_top(attend)
                        if s == DVE_AT["weigh_top"]:
                            weigh_top(attend)
                    if embed is not None:
                        if s == DVE_AT["tokens"]:
                            make_tokens(embed)
                        if s == DVE_AT["stats1"]:
                            stats1(embed)
                        if s == DVE_AT["normalise1"]:
                            normalise1(embed)

            def last(chunk):
                weigh_pair(chunk, PAIRS - 1)
                make_result(chunk)

            run_pipeline(dve, step, last)


_INS = ['x', 'L0_tok_W', 'L0_tok_b', 'L0_tok_pos_embed', 'L0_attn_w_qkv', 'L0_attn_b_qkv', 'L0_attn_w_proj',
        'L0_attn_b_proj', 'L0_ffn_gate_w', 'L0_ffn_gate_b', 'L0_ffn_w1', 'L0_ffn_w2', 'L0_ffn_w3']
_OUTS = [((4, 1024, 64), 'float32')]


def kernel(**inputs):
    import numpy as _np
    import concourse.bacc as _bacc
    from concourse import mybir as _mybir
    from concourse.bass_utils import run_bass_kernel_spmd as _run

    nc = _bacc.Bacc("TRN2", target_bir_lowering=False, num_devices=1)
    arrays, args = {}, []
    for name in _INS:
        a = _np.ascontiguousarray(inputs[name])
        arrays[f"in_{name}_dram"] = a
        args.append(nc.dram_tensor(f"in_{name}_dram", a.shape, _mybir.dt.from_np(a.dtype), kind="ExternalInput").ap())
    for i, (shape, dtype) in enumerate(_OUTS):
        dt = _mybir.dt.from_np(_np.dtype(dtype))
        args.append(nc.dram_tensor(f"out_{i}_dram", shape, dt, kind="ExternalOutput").ap())
    vit_tower(nc, *args)
    r = _run(nc, [arrays], core_ids=[0])
    return r.results[0]["out_0_dram"]
```
